# Optimizing a Trainium2 kernel written in Bass

```python
import numpy as np
import jax
import jax.numpy as jnp

def _softmax(x, axis=-1):
    return jax.nn.softmax(x, axis=axis)

def _gelu(x):
    return jax.nn.gelu(x, approximate=True)

def _silu(x):
    return jax.nn.silu(x)

def _sigmoid(x):
    return jax.nn.sigmoid(x)

def _layernorm(x, axis=-1, eps=1e-05):
    m = jnp.mean(x, axis=axis, keepdims=True)
    v = jnp.var(x, axis=axis, keepdims=True)
    return (x - m) / jnp.sqrt(v + eps)

def _scatter_add(tgt, idx, src, axis=0):
    return tgt.at[idx].add(src)

def _segment_sum(src, seg, n):
    return jax.ops.segment_sum(src, seg, n)
kernel_name = 'mk_decoder_postln_d1_seqx_r8_8b29e0'

def setup_inputs(seed: int=0):
    np.random.seed(seed)
    _w = jnp.asarray

    def _rec_inputs():
        import jax
        import jax.numpy as jnp
        _rk = jax.random.key(seed)
        x = -0.000125 + 0.9999 * jax.random.normal(jax.random.fold_in(_rk, 1), (4, 256, 256), jnp.float32)
        _lenS = 256 - jax.random.randint(jax.random.fold_in(_rk, 7), (4,), 0, max(1, 256 // 4) + 1, jnp.int32)
        _lenS2 = 256 - jax.random.randint(jax.random.fold_in(_rk, 8), (4,), 0, max(1, 256 // 4) + 1, jnp.int32)
        itok_BxS_13_99985 = jax.random.randint(jax.random.fold_in(_rk, 11), (4, 256), 13, 99986, jnp.int32)
        _ctx_2048P = jax.random.normal(jax.random.fold_in(_rk, 12), (4, 16, 256), jnp.float32)
        _ctx_2048c = jax.random.dirichlet(jax.random.fold_in(_rk, 512), 0.3 * jnp.ones((16,), jnp.float32), (4, 256))
        _ctx_2048t = jnp.einsum('bsk,bkd->bsd', _ctx_2048c, _ctx_2048P)
        _ctx_2048t = _ctx_2048t * jax.lax.rsqrt(jnp.mean(jnp.square(_ctx_2048t)) + 1e-12) * 0.953939
        ctx_2048 = 6.82029e-06 + 0.0200006 * (_ctx_2048t + 0.3 * jax.random.normal(jax.random.fold_in(_rk, 612), (4, 256, 256), jnp.float32))
        return (x, itok_BxS_13_99985, ctx_2048)
    x, itok_BxS_13_99985, ctx_2048 = _rec_inputs()

    def _L0_attn_setup():
        import jax, jax.numpy as jnp
        import numpy as np
        N_EMBD = 256
        N_HEAD = 16
        N_KV_HEAD = 4
        HEAD_DIM = N_EMBD // N_HEAD
        N_REP = N_HEAD // N_KV_HEAD
        ROPE_BASE = 1000000.0
        B, T = (2, 256)

        def _rotate_half(x):
            x1, x2 = jnp.split(x, 2, axis=-1)
            return jnp.concatenate([-x2, x1], axis=-1)

        def _rope(q, k, t):
            pos = jnp.arange(t, dtype=jnp.float32)
            inv_freq = 1.0 / ROPE_BASE ** (jnp.arange(0, HEAD_DIM, 2, dtype=jnp.float32) / HEAD_DIM)
            ang = pos[:, None] * inv_freq[None, :]
            cos = jnp.concatenate([jnp.cos(ang), jnp.cos(ang)], -1)
            sin = jnp.concatenate([jnp.sin(ang), jnp.sin(ang)], -1)
            cos = cos[None, :, None, :]
            sin = sin[None, :, None, :]
            q = q * cos + _rotate_half(q) * sin
            k = k * cos + _rotate_half(k) * sin
            return (q, k)
        key = jax.random.key(seed)
        ks = jax.random.split(key, 9)
        std = 0.02
        proj_std = 0.02 / np.sqrt(2 * 24)
        return {'x': jax.random.normal(ks[0], (B, T, N_EMBD), dtype=jnp.float32), 'Wq': jax.random.normal(ks[1], (N_EMBD, N_HEAD * HEAD_DIM), dtype=jnp.float32) * std, 'bq': jnp.zeros((N_HEAD * HEAD_DIM,), dtype=jnp.float32), 'Wk': jax.random.normal(ks[2], (N_EMBD, N_KV_HEAD * HEAD_DIM), dtype=jnp.float32) * std, 'bk': jnp.zeros((N_KV_HEAD * HEAD_DIM,), dtype=jnp.float32), 'Wv': jax.random.normal(ks[3], (N_EMBD, N_KV_HEAD * HEAD_DIM), dtype=jnp.float32) * std, 'bv': jnp.zeros((N_KV_HEAD * HEAD_DIM,), dtype=jnp.float32), 'Wo': jax.random.normal(ks[4], (N_EMBD, N_EMBD), dtype=jnp.float32) * proj_std, 'bo': jnp.zeros((N_EMBD,), dtype=jnp.float32)}
    _L0_attn_all = _L0_attn_setup()
    _L0_attn_in = {k: v for k, v in _L0_attn_all.items() if k in ('Wq', 'bq', 'Wk', 'bk', 'Wv', 'bv', 'Wo', 'bo')}
    del _L0_attn_all

    def _L0_xattn_setup():
        import jax, jax.numpy as jnp
        import numpy as np
        B, S, D = (4, 512, 256)
        E = 4
        F = 1024 // E
        VOCAB = 12500
        key = jax.random.key(seed)
        k1, k2, k3, k4, k5 = jax.random.split(key, 5)
        hidden_states = jax.random.normal(k1, (B, S, D), dtype=jnp.float32)
        token_ids = jax.random.randint(k2, (B, S), 0, VOCAB, dtype=jnp.int64)
        Wg = jax.random.normal(k3, (E, F, D), dtype=jnp.float32) * 0.02
        Wu = jax.random.normal(k4, (E, F, D), dtype=jnp.float32) * 0.02
        Wd = jax.random.normal(k5, (E, D, F), dtype=jnp.float32) * 0.02
        return {'hidden_states': hidden_states, 'token_ids': token_ids, 'Wg': Wg, 'Wu': Wu, 'Wd': Wd}
    _L0_xattn_all = _L0_xattn_setup()
    _L0_xattn_in = {k: v for k, v in _L0_xattn_all.items() if k in ()}
    del _L0_xattn_all

    def _L0_ffn_setup():
        import jax, jax.numpy as jnp
        import numpy as np
        DIM = 256
        N_EXPERTS = 8
        TOP_K = 2
        key = jax.random.key(seed)
        ks = jax.random.split(key, 5)
        x = jax.random.normal(ks[0], (4, 512, DIM), dtype=jnp.float32)
        W_up = jax.random.normal(ks[1], (DIM, DIM), dtype=jnp.float32) * (1.0 / np.sqrt(DIM))
        W_down = jax.random.normal(ks[2], (DIM, DIM), dtype=jnp.float32) * (1.0 / np.sqrt(DIM))
        W_gate = jax.random.normal(ks[3], (N_EXPERTS, DIM), dtype=jnp.float32) * (1.0 / np.sqrt(DIM))
        W_expert = jax.random.normal(ks[4], (DIM, DIM), dtype=jnp.float32) * (1.0 / np.sqrt(DIM))
        return {'x': x, 'W_up': W_up, 'W_down': W_down, 'W_gate': W_gate, 'W_expert': W_expert}
    _L0_ffn_all = _L0_ffn_setup()
    _L0_ffn_in = {k: v for k, v in _L0_ffn_all.items() if k in ('W_up', 'W_down', 'W_gate', 'W_expert')}
    del _L0_ffn_all
    return {'x': x, 'itok_BxS_13_99985': itok_BxS_13_99985, 'ctx_2048': ctx_2048, 'L0_attn_Wq': _L0_attn_in['Wq'], 'L0_attn_bq': _L0_attn_in['bq'], 'L0_attn_Wk': _L0_attn_in['Wk'], 'L0_attn_bk': _L0_attn_in['bk'], 'L0_attn_Wv': _L0_attn_in['Wv'], 'L0_attn_bv': _L0_attn_in['bv'], 'L0_attn_Wo': _L0_attn_in['Wo'], 'L0_attn_bo': _L0_attn_in['bo'], 'L0_ffn_W_up': _L0_ffn_in['W_up'], 'L0_ffn_W_down': _L0_ffn_in['W_down'], 'L0_ffn_W_gate': _L0_ffn_in['W_gate'], 'L0_ffn_W_expert': _L0_ffn_in['W_expert']}

def reference(x, itok_BxS_13_99985, ctx_2048, L0_attn_Wq, L0_attn_bq, L0_attn_Wk, L0_attn_bk, L0_attn_Wv, L0_attn_bv, L0_attn_Wo, L0_attn_bo, L0_ffn_W_up, L0_ffn_W_down, L0_ffn_W_gate, L0_ffn_W_expert):
    import jax
    import jax.numpy as jnp

    def _L0_attn_ref(x, Wq, bq, Wk, bk, Wv, bv, Wo, bo):
        import jax, jax.numpy as jnp
        import numpy as np
        N_EMBD = 256
        N_HEAD = 16
        N_KV_HEAD = 4
        HEAD_DIM = N_EMBD // N_HEAD
        N_REP = N_HEAD // N_KV_HEAD
        ROPE_BASE = 1000000.0
        B, T = (2, 256)

        def _rotate_half(x):
            x1, x2 = jnp.split(x, 2, axis=-1)
            return jnp.concatenate([-x2, x1], axis=-1)

        def _rope(q, k, t):
            pos = jnp.arange(t, dtype=jnp.float32)
            inv_freq = 1.0 / ROPE_BASE ** (jnp.arange(0, HEAD_DIM, 2, dtype=jnp.float32) / HEAD_DIM)
            ang = pos[:, None] * inv_freq[None, :]
            cos = jnp.concatenate([jnp.cos(ang), jnp.cos(ang)], -1)
            sin = jnp.concatenate([jnp.sin(ang), jnp.sin(ang)], -1)
            cos = cos[None, :, None, :]
            sin = sin[None, :, None, :]
            q = q * cos + _rotate_half(q) * sin
            k = k * cos + _rotate_half(k) * sin
            return (q, k)
        b, t, _ = x.shape
        q = (x @ Wq + bq).reshape(b, t, N_HEAD, HEAD_DIM)
        k = (x @ Wk + bk).reshape(b, t, N_KV_HEAD, HEAD_DIM)
        v = (x @ Wv + bv).reshape(b, t, N_KV_HEAD, HEAD_DIM)
        q, k = _rope(q, k, t)
        k = jnp.broadcast_to(k[:, :, :, None, :], (b, t, N_KV_HEAD, N_REP, HEAD_DIM)).reshape(b, t, N_HEAD, HEAD_DIM)
        v = jnp.broadcast_to(v[:, :, :, None, :], (b, t, N_KV_HEAD, N_REP, HEAD_DIM)).reshape(b, t, N_HEAD, HEAD_DIM)
        qh = q.transpose(0, 2, 1, 3)
        kh = k.transpose(0, 2, 1, 3)
        vh = v.transpose(0, 2, 1, 3)
        causal = jnp.tril(jnp.ones((t, t), dtype=bool))[None, None]
        bias = jnp.where(causal, 0.0, -1000000000.0).astype(jnp.float32)
        scores = jnp.einsum('bhtd,bhTd->bhtT', qh, kh) / jnp.sqrt(jnp.float32(HEAD_DIM))
        attn_w = jax.nn.softmax(scores + bias, axis=-1)
        attn_out = jnp.einsum('bhtT,bhTd->bhtd', attn_w, vh)
        attn = attn_out.transpose(0, 2, 1, 3).reshape(b, t, N_EMBD)
        return attn @ Wo + bo

    def _L0_xattn_ref(hidden_states, token_ids, Wg, Wu, Wd):
        import jax, jax.numpy as jnp
        import numpy as np
        B, S, D = (4, 512, 256)
        E = 4
        F = 1024 // E
        VOCAB = 12500
        tokens_per_expert = VOCAB // E
        tid = jnp.clip(token_ids, 0, VOCAB - 1)
        expert_ids = jnp.minimum(tid // tokens_per_expert, E - 1)
        out = jnp.zeros_like(hidden_states)
        for e in range(E):
            g = jax.nn.silu(jnp.einsum('bsd,fd->bsf', hidden_states, Wg[e]))
            u = jnp.einsum('bsd,fd->bsf', hidden_states, Wu[e])
            y = jnp.einsum('bsf,df->bsd', g * u, Wd[e])
            out = jnp.where((expert_ids == e)[..., None], y, out)
        return out

    def _L0_ffn_ref(x, W_up, W_down, W_gate, W_expert):
        import jax, jax.numpy as jnp
        import numpy as np
        DIM = 256
        N_EXPERTS = 8
        TOP_K = 2
        logits = jnp.einsum('bsd,ed->bse', x, W_gate)
        routing_weights, selected_experts = jax.lax.top_k(logits, TOP_K)
        shared_out = jnp.einsum('bsd,od->bso', jax.nn.relu(jnp.einsum('bsd,od->bso', x, W_up)), W_down)
        rw = jax.nn.softmax(routing_weights, axis=-1)
        expert_out = jnp.einsum('bsd,do->bso', x, W_expert)
        moe_out = jnp.sum(rw, axis=-1, keepdims=True) * expert_out
        return shared_out + moe_out
    x = _layernorm(x + _L0_attn_ref(x, L0_attn_Wq, L0_attn_bq, L0_attn_Wk, L0_attn_bk, L0_attn_Wv, L0_attn_bv, L0_attn_Wo, L0_attn_bo), axis=-1)
    x = _layernorm(x + _L0_xattn_ref(x, itok_BxS_13_99985, ctx_2048, ctx_2048, ctx_2048), axis=-1)
    x = _layernorm(x + _L0_ffn_ref(x, L0_ffn_W_up, L0_ffn_W_down, L0_ffn_W_gate, L0_ffn_W_expert), axis=-1)
    return x

_drawn_inputs = setup_inputs


def setup_inputs(seed=0):
    import zlib

    import numpy as np

    out = dict(_drawn_inputs(seed))
    spreads = {'L0_attn_bq': (0.0, 0.8),
     'L0_attn_bk': (0.0, 0.8),
     'L0_attn_bv': (0.0, 0.8),
     'L0_attn_bo': (0.0, 0.1)}
    factors = {'L0_attn_Wq': 8.0,
     'L0_attn_Wk': 8.0,
     'L0_attn_Wv': 8.0,
     'L0_attn_Wo': 8.0,
     'L0_ffn_W_gate': 8.0}
    for name, (base, spread) in spreads.items():
        noise = np.random.default_rng([zlib.crc32(name.encode()), seed]).standard_normal(out[name].shape)
        drawn = base * np.exp(spread * noise) if base else spread * noise
        out[name] = jnp.asarray(drawn.astype(out[name].dtype))
    for name, factor in factors.items():
        out[name] = (out[name] * factor).astype(out[name].dtype)
    return out
```

```python
from contextlib import ExitStack

import numpy as np

import concourse.bass as bass
from concourse import mybir

F32 = mybir.dt.float32
F32R = mybir.dt.float32r
BF16 = mybir.dt.bfloat16
I32 = mybir.dt.int32
ALU = mybir.AluOpType
ACT = mybir.ActivationFunctionType
AX = mybir.AxisListType

P = 128
B, S, D = 4, 256, 256
NT = S // P
ND = D // P
H, G = 16, 4
R = H // G
HD = D // H
KVW = G * HD
E = 4
VOCAB = 12500
TPE = VOCAB // E
NG = 8
EPS = 1e-5
MASK = -4.0e9
SCALE = float(HD) ** -0.5
QPARTS = (0, 0, 0, 1, 1, 2)
KPARTS = (0, 1, 2, 0, 1, 0)
NPART = len(QPARTS)
KQ = NPART * HD
HB = P // HD
NQB = H // HB
UNITS = 3
VW = 2 * HD


def steps():
    yield from (("project", 0, i) for i in range(4))
    yield from (("project", 1, i) for i in range(4))
    yield from (("max", 0, j) for j in range(G))
    yield "maxrow", 0, 0
    for b in range(B):
        for j in range(G):
            yield "probs", b, j
            if b + 1 < B:
                yield "max", b + 1, j
            if j:
                yield "pv", b, j - 1
        yield "pv", b, G - 1
        if b + 1 < B:
            yield "maxrow", b + 1, 0
        for t in range(NT):
            yield "heads", b, t
            if b + 2 < B:
                yield "project", b + 2, 2 * t
            yield "wo", b, t
            if b + 2 < B:
                yield "project", b + 2, 2 * t + 1
        for t in range(NT):
            yield "x1t", b, t
        for e in range(E):
            yield "expert", b, e
            if e:
                yield "down", b, e - 1
        yield "down", b, E - 1
        for t in range(NT):
            yield "x2t", b, t
        yield "up", b, 0
        for t in range(NT):
            yield "gate", b, t
        for t in range(NT):
            yield "ffn", b, t


SHARED_USES = {"project": 1, "maxrow": 1, "heads": 2, "wo": 1, "x1t": 1, "expert": 1, "x2t": 1,
               "up": 1, "gate": 1, "ffn": 1}


def shared_use():
    n, first = 0, {}
    for s in steps():
        first[s] = n
        n += SHARED_USES.get(s[0], 0)
    return first


def decoder_layer(nc, a):
    first_use = shared_use()
    with ExitStack() as ctx:
        def sb(name, shape, dt=F32):
            return ctx.enter_context(nc.sbuf_tensor(name, shape, dt))

        def bank(name, shape):
            return ctx.enter_context(nc.psum_tensor(name, shape, F32))

        def sem(name):
            return ctx.enter_context(nc.semaphore(name))

        ident = sb("ident", [P, P])
        ident_bf = sb("ident_bf", [P, P], BF16)
        causal = sb("causal", [P, R, P], BF16)
        cos, sin = sb("cos", [P, S]), sb("sin", [P, S])
        rope_k = sb("rope_k", [P, S])
        w_qk = sb("w_qk", [P, ND, 5 * P])
        w_qk_hi, w_qk_lo = sb("w_qk_hi", [P, ND, 5 * P], F32R), sb("w_qk_lo", [P, ND, 5 * P], F32R)
        b_qk = sb("b_qk", [P, 5])
        w_v = sb("w_v", [P, ND, KVW])
        bv_all = sb("bv_all", [P, NT, KVW])
        w_o = sb("w_o", [P, ND, D])
        bo_all = sb("bo_all", [P, D])
        w_ex = sb("w_ex", [P, ND, E, D])
        w_ex_hi, w_ex_lo = sb("w_ex_hi", [P, ND, E, D], F32R), sb("w_ex_lo", [P, ND, E, D], F32R)
        w_up = sb("w_up", [P, ND, D])
        w_up_hi, w_up_lo = sb("w_up_hi", [P, ND, D], F32R), sb("w_up_lo", [P, ND, D], F32R)
        w_gx = sb("w_gx", [P, ND, D + NG])
        w_gx_hi, w_gx_lo = sb("w_gx_hi", [P, ND, D + NG], F32R), sb("w_gx_lo", [P, ND, D + NG], F32R)
        w_dn = sb("w_dn", [P, ND, D])
        half_power = sb("half_power", [P, NT])
        tok = sb("tok", [P, B * S], I32)
        route = sb("route", [P, E, B * S], BF16)
        x_bo = sb("x_bo", [P, B * NT, D])
        xt = sb("xt", [P, ND, B, S])
        xt_hi, xt_lo = sb("xt_hi", [P, ND, 2, S], F32R), sb("xt_lo", [P, ND, 2, S], F32R)
        rc, rs = sb("rc", [P, 2, S]), sb("rs", [P, 2, S])
        qk_rot, qk_rest = sb("qk_rot", [P, 3, S]), sb("qk_rest", [P, 3, S])
        qk_parts = sb("qk_parts", [P, 3, 3, S], BF16)
        q_st = sb("q_st", [KQ + 1, 2, H, S], BF16)
        k_st = sb("k_st", [KQ + 1, 2, G, S], BF16)
        v_st = sb("v_st", [P, 2, NT, G, VW])
        mx = sb("mx", [P, 2, NT, H])
        neg_mx = sb("neg_mx", [H, 2, S], BF16)
        probs = sb("probs", [P, 2 * UNITS, R * P])
        heads_t = sb("heads_t", [P, NT, R * P])
        rden = sb("rden", [P, NT, R, G])
        attn = sb("attn", [P, NT, D])
        attn_t = sb("attn_t", [P, NT, ND, P])
        z = sb("z", [P, NT, D])
        stats = sb("stats", [P, NT, 6])
        mv = sb("mv", [P, NT, 2])
        veps, rstd = sb("veps", [P, NT]), sb("rstd", [P, NT])
        x1, x2 = sb("x1", [P, NT, D]), sb("x2", [P, NT, D])
        x1t_hi, x1t_lo = sb("x1t_hi", [P, ND, S], F32R), sb("x1t_lo", [P, ND, S], F32R)
        x2t_hi, x2t_lo = sb("x2t_hi", [P, ND, S], F32R), sb("x2t_lo", [P, ND, S], F32R)
        th, sq = sb("th", [P, 2, ND, S]), sb("sq", [P, 2, ND, S])
        hid = sb("hid", [P, 2, ND, S])
        up_t = sb("up_t", [P, ND, S])
        top = sb("top", [P, NT, 8])
        gd, ge, gs, gr, gw, gt = (sb(n, [P, NT]) for n in ("gd", "ge", "gs", "gr", "gw", "gt"))
        moe, moe_x = sb("moe", [P, NT, D]), sb("moe_x", [P, NT, D])
        y_out = sb("y_out", [P, 2, NT, D])

        max_ps = [bank(f"max_ps{i}", [P, 512]) for i in range(2)]
        sc_ps = [bank(f"sc_ps{i}", [P, 512]) for i in range(2)]
        acc_ps = [bank(f"acc_ps{t}", [P, 512]) for t in range(NT)]
        shared = [bank(f"shared{i}", [P, 512]) for i in range(2)]

        ld = {n: sem("ld_" + n) for n in ("w_qk", "tabs", "w_v", "mask", "tok", "w_o", "w_ex", "w_ffn", "x")}
        ld_xt = [sem(f"ld_xt{b}") for b in range(B)]
        names = ("w_qk_hi w_qk_lo xt_hi xt_lo w_ex_hi w_ex_lo w_ffn_hi w_ffn_lo consts route_ge route_mid "
                 "route_done x_bo_done proj_mm v_mm rope_cos rot_done hi_part rest_done mid_part parts_done "
                 "max_mm max_red mxt_mm score_mm exp_done masked_done pv_mm heads_copied heads_mm "
                 "rden_done attn_mm wo_mm stats_done mv_done veps_done rstd_done x1_done x1t_mm x1t_hi_done "
                 "gate_mm tanh_done sqr_done hid_done down_mm z2_done x2_done x2t_mm x2t_hi_done up_mm "
                 "gx_mm top_done gdiff_done gexp_done gsum_done grec_done gw_done moe_x_done ffn_mm "
                 "y_done").split()
        s = {n: sem(n) for n in names}
        qk_moved = [sem(f"qk_moved{i}") for i in range(2)]
        mx_moved = [sem(f"mx_moved{i}") for i in range(2)]
        stored = [sem(f"stored{i}") for i in range(2)]
        shared_read = [sem(f"shared_read{i}") for i in range(2)]

        NDMA_QK = 16 * NPART * 3

        def take_shared(pe, step, k=0):
            n = first_use[step] + k
            if n >= 2:
                pe.wait_ge(shared_read[n % 2], n // 2)
            return shared[n % 2]

        def shared_of(step, k=0):
            n = first_use[step] + k
            return shared[n % 2], shared_read[n % 2], n // 2 + 1

        def wait_shared(eng, step, k=0):
            _, read, value = shared_of(step, k)
            eng.wait_ge(read, value)

        def three_pass(pe, out, w_hi, w_lo, m_hi, m_lo):
            n = len(w_hi)
            for k in range(n):
                pe.matmul(out, w_hi[k], m_hi[k], start=(k == 0), stop=False)
                pe.matmul(out, w_hi[k], m_lo[k], start=False, stop=False)
                last = pe.matmul(out, w_lo[k], m_hi[k], start=False, stop=(k == n - 1))
            return last

        block = ctx.enter_context(nc.Block())

        @block.sync
        def _(sp):
            def load(dst, src, signal):
                sp.dma_start(dst, src).then_inc(signal, 16)

            load(w_qk[:, :, :], a["w_qk"].rearrange("(k p) n -> p k n", p=P), ld["w_qk"])
            xt_view = a["x_t"].rearrange("(k p) (b s) -> p k b s", p=P, b=B)
            load(xt[:, :, 0, :], xt_view[:, :, 0, :], ld_xt[0])
            load(cos[:, :], a["cos"], ld["tabs"])
            load(sin[:, :], a["sin"], ld["tabs"])
            load(rope_k[:, :], a["rope_k"], ld["tabs"])
            load(b_qk[:, :], a["b_qk"], ld["tabs"])
            load(w_v[:, :, :], a["w_v"].rearrange("(k p) n -> p k n", p=P), ld["w_v"])
            load(bv_all[:, :, :], a["b_v"].rearrange("(o t n) -> o t n", o=1, t=1).to_broadcast([P, NT, KVW]),
                 ld["w_v"])
            load(xt[:, :, 1, :], xt_view[:, :, 1, :], ld_xt[1])
            load(causal[:, :, :], a["causal"].rearrange("p (r k) -> p r k", r=R), ld["mask"])
            load(ident_bf[:, :], a["ident_bf"], ld["mask"])
            load(ident[:, :], a["ident"], ld["mask"])
            load(tok[:, :], a["tok"].rearrange("b s -> (b s)").rearrange("(o n) -> o n", o=1)
                 .to_broadcast([P, B * S]), ld["tok"])
            load(w_ex[:, :, :, :], a["w_ex"].rearrange("(k p) (e f) -> p k e f", p=P, e=E), ld["w_ex"])
            load(x_bo[:, :, :], a["x"].rearrange("(t p) d -> p t d", p=P), ld["x"])
            load(bo_all[:, :], a["b_o"].rearrange("(o n) -> o n", o=1).to_broadcast([P, D]), ld["x"])
            load(w_o[:, :, :], a["w_o"].rearrange("(k p) n -> p k n", p=P), ld["w_o"])
            for b in range(2, B):
                load(xt[:, :, b, :], xt_view[:, :, b, :], ld_xt[b])
            load(w_up[:, :, :], a["w_up"].rearrange("(k p) n -> p k n", p=P), ld["w_ffn"])
            load(w_gx[:, :, :], a["w_gx"].rearrange("(k p) n -> p k n", p=P), ld["w_ffn"])
            load(w_dn[:, :, :], a["w_dn"].rearrange("(k p) n -> p k n", p=P), ld["w_ffn"])

            for step in steps():
                name, b, i = step
                c = b % 2
                if name == "project" and i < 3:
                    if i == 0 and b >= 2:
                        sp.wait_ge(s["score_mm"], UNITS * G * (b - 1))
                    sp.wait_ge(s["parts_done"], 3 * b + i + 1)
                    for n in range(NPART):
                        rows = slice(n * HD, (n + 1) * HD)
                        if i < NQB:
                            dst = q_st[rows, c, HB * i:HB * (i + 1), :]
                            src = qk_parts[:, i, QPARTS[n], :]
                        else:
                            dst = k_st[rows, c, :, :]
                            src = qk_parts[0:KVW, i, KPARTS[n], :]
                        sp.dma_start(dst, src).then_inc(qk_moved[c], 16)
                elif name == "maxrow":
                    wait_shared(sp, step)
                    sp.dma_start(q_st[KQ:KQ + 1, c, :, :], neg_mx[:, c, :]).then_inc(mx_moved[c], 16)
                elif name == "ffn":
                    sp.wait_ge(s["y_done"], NT * b + i + 1)
                    t = NT * b + i
                    sp.dma_start(a["out"][t * P:(t + 1) * P, :], y_out[:, c, i, :]).then_inc(stored[c], 16)
            sp.wait_ge(stored[0], 16 * NT * 2)
            sp.wait_ge(stored[1], 16 * NT * 2)

        @block.tensor
        def _(pe):
            for step in steps():
                name, b, i = step
                c = b % 2
                if name == "project":
                    ps = take_shared(pe, step)
                    if i < 3:
                        pe.wait_ge(s["w_qk_lo"], 1)
                        pe.wait_ge(s["xt_lo"], b + 1)
                        for n in range(2 if i < NQB else 1):
                            cols = slice((2 * i + n) * P, (2 * i + n + 1) * P)
                            last = three_pass(pe, ps[:, n * S:(n + 1) * S],
                                              [w_qk_hi[:, k, cols] for k in range(ND)],
                                              [w_qk_lo[:, k, cols] for k in range(ND)],
                                              [xt_hi[:, k, c, :] for k in range(ND)],
                                              [xt_lo[:, k, c, :] for k in range(ND)])
                        last.then_inc(s["proj_mm"], 1)
                    else:
                        pe.wait_ge(ld["w_v"], 32)
                        pe.wait_ge(ld_xt[b], 16)
                        for t in range(NT):
                            for k in range(ND):
                                last = pe.matmul(ps[:, t * KVW:(t + 1) * KVW],
                                                 xt[:, k, b, t * P:(t + 1) * P], w_v[:, k, :],
                                                 start=(k == 0), stop=(k == ND - 1))
                        last.then_inc(s["v_mm"], 1)
                elif name == "max":
                    if i == 0:
                        pe.wait_ge(qk_moved[c], NDMA_QK * (b // 2 + 1))
                        pe.wait_ge(ld["mask"], 48)
                    for u in range(UNITS):
                        n = UNITS * (G * b + i) + u
                        if n >= 2:
                            pe.wait_ge(s["max_red"], n - 1)
                        ps = max_ps[n % 2]
                        if u == 0:
                            out = ps[:, :].rearrange("p (h k) -> p h k", h=R)
                            pe.matmul(out, ident_bf[:, :], causal[:, :, :], start=True, stop=False,
                                      skip_group_check=True)
                            hs, q0, nk = range(R), 0, P
                        else:
                            out = ps[:, :].rearrange("p (h k) -> p h k", h=2)
                            pe.matmul(out[:, :, P:S], ident_bf[:, :], causal[:, 0:2, :],
                                      start=True, stop=False, skip_group_check=True)
                            hs, q0, nk = range(2 * (u - 1), 2 * u), P, S
                        for m, h in enumerate(hs):
                            last = pe.matmul(out[:, m, :], q_st[0:KQ, c, R * i + h, q0:q0 + P],
                                             k_st[0:KQ, c, i, 0:nk], start=False, stop=(h == hs[-1]),
                                             skip_group_check=True)
                        last.then_inc(s["max_mm"], 1)
                elif name == "maxrow":
                    ps = take_shared(pe, step)
                    pe.wait_ge(s["max_red"], UNITS * G * (b + 1))
                    for t in range(NT):
                        last = pe.transpose(ps[0:H, t * P:(t + 1) * P], mx[:, c, t, :], ident[:, :])
                    last.then_inc(s["mxt_mm"], 1)
                elif name == "probs":
                    if i == 0:
                        pe.wait_ge(mx_moved[c], 16 * (b // 2 + 1))
                        pe.wait_ge(s["consts"], 3)
                    for u, (t, k) in enumerate(((0, 0), (1, 0), (1, 1))):
                        n = UNITS * (G * b + i) + u
                        if n >= 2:
                            pe.wait_ge(s["exp_done"], n - 1)
                        pe.matmul(sc_ps[n % 2][:, :], k_st[:, c, i, k * P:(k + 1) * P],
                                  q_st[:, c, R * i:R * (i + 1), t * P:(t + 1) * P],
                                  start=True, stop=True).then_inc(s["score_mm"], 1)
                elif name == "pv":
                    if i == 0:
                        wait_shared(pe, ("project", b, 3))
                        if b:
                            pe.wait_ge(s["z2_done"], NT * b)
                    for u, (t, k) in enumerate(((0, 0), (1, 0), (1, 1))):
                        n = UNITS * (G * b + i) + u
                        if u == 1:
                            pe.wait_ge(s["exp_done"], n + 1)
                        else:
                            pe.wait_ge(s["masked_done"], 2 * (G * b + i) + (u > 0) + 1)
                        last = pe.matmul(acc_ps[t][32 * i:32 * i + VW, :], v_st[:, c, k, i, :],
                                         probs[:, n % (2 * UNITS), :], start=(k == 0), stop=(k == t),
                                         tile_position=(0, 32 * i))
                    last.then_inc(s["pv_mm"], 1)
                elif name == "heads":
                    n = NT * b + i
                    ps = take_shared(pe, step)
                    pe.wait_ge(s["heads_copied"], n + 1)
                    for r in range(R):
                        last = pe.transpose(ps[:, r * P:(r + 1) * P], heads_t[:, i, r * P:(r + 1) * P],
                                            ident[:, :])
                    last.then_inc(s["heads_mm"], 1)
                    ps = take_shared(pe, step, 1)
                    wait_shared(pe, step)
                    for k in range(ND):
                        last = pe.transpose(ps[:, k * P:(k + 1) * P], attn[:, i, k * P:(k + 1) * P],
                                            ident[:, :])
                    last.then_inc(s["attn_mm"], 1)
                elif name == "wo":
                    ps = take_shared(pe, step)
                    wait_shared(pe, ("heads", b, i), 1)
                    pe.wait_ge(ld["w_o"], 16)
                    for k in range(ND):
                        last = pe.matmul(ps[:, 0:D], attn_t[:, i, k, :], w_o[:, k, :],
                                         start=(k == 0), stop=(k == ND - 1))
                    last.then_inc(s["wo_mm"], 1)
                elif name in ("x1t", "x2t"):
                    src = x1 if name == "x1t" else x2
                    ps = take_shared(pe, step)
                    pe.wait_ge(s[name[:2] + "_done"], NT * b + i + 1)
                    for k in range(ND):
                        last = pe.transpose(ps[:, k * P:(k + 1) * P], src[:, i, k * P:(k + 1) * P],
                                            ident[:, :])
                    last.then_inc(s[name + "_mm"], 1)
                elif name == "expert":
                    ps = take_shared(pe, step)
                    pe.wait_ge(s["w_ex_lo"], 1)
                    for t in range(NT):
                        wait_shared(pe, ("x1t", b, t))
                    for m in range(ND):
                        cols = slice(m * P, (m + 1) * P)
                        last = three_pass(pe, ps[:, m * S:(m + 1) * S],
                                          [w_ex_hi[:, k, i, cols] for k in range(ND)],
                                          [w_ex_lo[:, k, i, cols] for k in range(ND)],
                                          [x1t_hi[:, k, :] for k in range(ND)],
                                          [x1t_lo[:, k, :] for k in range(ND)])
                    last.then_inc(s["gate_mm"], 1)
                elif name == "down":
                    n = E * b + i
                    pe.wait_ge(s["hid_done"], n + 1)
                    if i == 0:
                        pe.wait_ge(s["heads_copied"], NT * (b + 1))
                    for t in range(NT):
                        for k in range(ND):
                            last = pe.matmul(acc_ps[t][:, 0:D], hid[:, n % 2, k, t * P:(t + 1) * P],
                                             w_ex[:, k, i, :], start=(i == 0 and k == 0),
                                             stop=(i == E - 1 and k == ND - 1))
                    last.then_inc(s["down_mm"], 1)
                elif name == "up":
                    ps = take_shared(pe, step)
                    pe.wait_ge(s["w_ffn_lo"], 2)
                    for t in range(NT):
                        wait_shared(pe, ("x2t", b, t))
                    for m in range(ND):
                        cols = slice(m * P, (m + 1) * P)
                        last = three_pass(pe, ps[:, m * S:(m + 1) * S],
                                          [w_up_hi[:, k, cols] for k in range(ND)],
                                          [w_up_lo[:, k, cols] for k in range(ND)],
                                          [x2t_hi[:, k, :] for k in range(ND)],
                                          [x2t_lo[:, k, :] for k in range(ND)])
                    last.then_inc(s["up_mm"], 1)
                elif name == "gate":
                    ps = take_shared(pe, step)
                    tt = slice(i * P, (i + 1) * P)
                    three_pass(pe, ps[:, 0:D + NG],
                               [x2t_hi[:, k, tt] for k in range(ND)], [x2t_lo[:, k, tt] for k in range(ND)],
                               [w_gx_hi[:, k, :] for k in range(ND)], [w_gx_lo[:, k, :] for k in range(ND)],
                               ).then_inc(s["gx_mm"], 1)
                elif name == "ffn":
                    ps = take_shared(pe, step)
                    wait_shared(pe, ("up", b, 0))
                    for k in range(ND):
                        last = pe.matmul(ps[:, 0:D], up_t[:, k, i * P:(i + 1) * P], w_dn[:, k, :],
                                         start=(k == 0), stop=(k == ND - 1))
                    last.then_inc(s["ffn_mm"], 1)

        @block.scalar
        def _(act):
            act.wait_ge(ld["w_qk"], 16)
            act.activation(w_qk_hi[:, :, :], w_qk[:, :, :], ACT.Copy).then_inc(s["w_qk_hi"], 1)
            for step in steps():
                name, b, i = step
                c = b % 2
                if name == "probs":
                    for u in range(UNITS):
                        n = UNITS * (G * b + i) + u
                        act.wait_ge(s["score_mm"], n + 1)
                        if n >= 2 * UNITS:
                            act.wait_ge(s["pv_mm"], (n - 2 * UNITS) // UNITS + 1)
                        act.activation(probs[:, n % (2 * UNITS), :], sc_ps[n % 2][:, :], ACT.Exp,
                                       scale=SCALE).then_inc(s["exp_done"], 1)
                elif name == "maxrow":
                    ps, read, _ = shared_of(step)
                    act.wait_ge(s["mxt_mm"], b + 1)
                    if b >= 2:
                        act.wait_ge(mx_moved[c], 16 * (b // 2))
                    act.activation(neg_mx[:, c, :], ps[0:H, 0:S], ACT.Copy, scale=-1.0).then_inc(read, 1)
                elif name == "heads":
                    n = NT * b + i
                    act.wait_ge(s["pv_mm"], G * (b + 1))
                    if b:
                        act.wait_ge(s["heads_mm"], n - NT + 1)
                    act.activation(heads_t[:, i, :], acc_ps[i][:, :], ACT.Copy).then_inc(s["heads_copied"], 1)
                    ps, read, _ = shared_of(step, 1)
                    act.wait_ge(s["attn_mm"], n + 1)
                    if b:
                        act.wait_ge(s["wo_mm"], n - NT + 1)
                    act.activation(attn_t[:, i, :, :], ps[:, 0:D].rearrange("p (k q) -> p k q", k=ND),
                                   ACT.Copy).then_inc(read, 1)
                elif name in ("x1t", "x2t"):
                    ps, _, _ = shared_of(step)
                    act.wait_ge(s[name + "_mm"], NT * b + i + 1)
                    if b and name == "x1t":
                        act.wait_ge(s["gate_mm"], E * b)
                    if b and name == "x2t":
                        act.wait_ge(s["gx_mm"], NT * b)
                    hi = x1t_hi if name == "x1t" else x2t_hi
                    act.activation(hi[:, :, i * P:(i + 1) * P], ps[:, 0:D].rearrange("p (k q) -> p k q", k=ND),
                                   ACT.Copy).then_inc(s[name + "_hi_done"], 1)
                elif name == "expert":
                    n = E * b + i
                    ps, read, _ = shared_of(step)
                    act.wait_ge(s["gate_mm"], n + 1)
                    if n >= 2:
                        act.wait_ge(s["hid_done"], n - 1)
                    g = ps[:, :].rearrange("p (m q) -> p m q", m=ND)
                    act.activation(th[:, n % 2, :, :], g, ACT.Tanh, scale=0.5).then_inc(s["tanh_done"], 1)
                    act.activation(sq[:, n % 2, :, :], g, ACT.Square).then_inc(read, 1)
                elif name == "up":
                    ps, read, _ = shared_of(step)
                    act.wait_ge(s["up_mm"], b + 1)
                    if b:
                        act.wait_ge(s["ffn_mm"], NT * b)
                    act.activation(up_t[:, :, :], ps[:, :].rearrange("p (m q) -> p m q", m=ND),
                                   ACT.Relu).then_inc(read, 1)
                elif name == "gate":
                    n = NT * b + i
                    ps, read, _ = shared_of(step)
                    act.wait_ge(s["gdiff_done"], n + 1)
                    if b:
                        act.wait_ge(s["gw_done"], n - NT + 1)
                    act.activation(ge[:, i:i + 1], gd[:, i:i + 1], ACT.Exp).then_inc(s["gexp_done"], 1)
                    act.wait_ge(s["gw_done"], n + 1)
                    if b:
                        act.wait_ge(s["moe_x_done"], n - NT + 1)
                    act.activation(moe[:, i, :], ps[:, 0:D], ACT.Copy, scale=gw[:, i:i + 1]).then_inc(read, 1)

        @block.vector
        def _(dve):
            dve.memset(v_st[:, :, :, :, :], 1.0).then_inc(s["consts"], 1)
            dve.memset(half_power[:, :], -0.5).then_inc(s["consts"], 1)
            dve.memset(k_st[KQ:KQ + 1, :, :, :], 1.0).then_inc(s["consts"], 1)
            dve.wait_ge(s["w_qk_hi"], 1)
            dve.tensor_tensor(w_qk_lo[:, :, :], w_qk[:, :, :], w_qk_hi[:, :, :].bitcast(F32),
                              ALU.subtract).then_inc(s["w_qk_lo"], 1)
            norms = 0

            def layernorm(n, i, out, signal):
                dve.bn_stats(stats[:, i, :], z[:, i, :]).then_inc(s["stats_done"], 1)
                dve.wait_ge(s["stats_done"], n)
                dve.bn_aggr(mv[:, i, :], stats[:, i, :]).then_inc(s["mv_done"], 1)
                dve.wait_ge(s["mv_done"], n)
                dve.wait_ge(s["rstd_done"], n)
                dve.tensor_scalar(out, z[:, i, :], mv[:, i, 0:1], rstd[:, i:i + 1],
                                  ALU.subtract, ALU.mult).then_inc(signal, 1)

            for step in steps():
                name, b, i = step
                c = b % 2
                if name == "project":
                    ps, read, _ = shared_of(step)
                    if i == 0:
                        dve.wait_ge(s["xt_hi"], b + 1)
                        if b >= 2:
                            dve.wait_ge(s["proj_mm"], 3 * (b - 1))
                        dve.tensor_tensor(xt_lo[:, :, c, :], xt[:, :, b, :], xt_hi[:, :, c, :].bitcast(F32),
                                          ALU.subtract).then_inc(s["xt_lo"], 1)
                    if i < 3:
                        n = 3 * b + i
                        dve.wait_ge(s["proj_mm"], n + 1)
                        dve.wait_ge(ld["tabs"], 64)
                        if n >= 2:
                            dve.wait_ge(s["rot_done"], n - 1)
                    if i < NQB:
                        dve.scalar_tensor_tensor(out=rc[:, n % 2, :], in0=ps[:, 0:S],
                                                 scalar=b_qk[:, 2 * i:2 * i + 1], in1=cos[:, :],
                                                 op0=ALU.add, op1=ALU.mult).then_inc(s["rope_cos"], 1)
                        dve.scalar_tensor_tensor(out=rs[:, n % 2, :], in0=ps[:, S:2 * S],
                                                 scalar=b_qk[:, 2 * i + 1:2 * i + 2], in1=sin[:, :],
                                                 op0=ALU.add, op1=ALU.mult).then_inc(read, 1)
                    elif i == 2:
                        dve.scalar_tensor_tensor(out=rc[0:KVW, n % 2, :], in0=ps[0:KVW, 0:S],
                                                 scalar=b_qk[0:KVW, 4:5], in1=rope_k[0:KVW, :],
                                                 op0=ALU.add, op1=ALU.mult).then_inc(s["rope_cos"], 1)
                        dve.scalar_tensor_tensor(out=rs[0:KVW, n % 2, :], in0=ps[KVW:P, 0:S],
                                                 scalar=b_qk[KVW:P, 4:5], in1=rope_k[KVW:P, :],
                                                 op0=ALU.add, op1=ALU.mult).then_inc(read, 1)
                    else:
                        dve.wait_ge(s["v_mm"], b + 1)
                        dve.wait_ge(ld["w_v"], 32)
                        if b == 0:
                            dve.wait_ge(s["consts"], 1)
                        if b >= 2:
                            dve.wait_ge(s["pv_mm"], G * (b - 1))
                        dve.tensor_tensor(v_st[:, c, :, :, 0:HD],
                                          ps[:, 0:NT * KVW].rearrange("p (t g d) -> p t g d", t=NT, g=G),
                                          bv_all[:, :, :].rearrange("p t (g d) -> p t g d", g=G),
                                          ALU.add).then_inc(read, 1)
                elif name == "max":
                    if b >= 2 and i == 0:
                        dve.wait_ge(s["mxt_mm"], b - 1)
                    for u in range(UNITS):
                        n = UNITS * (G * b + i) + u
                        dve.wait_ge(s["max_mm"], n + 1)
                        h, nh = (R * i, R) if u == 0 else (R * i + 2 * (u - 1), 2)
                        dve.tensor_reduce(mx[:, c, int(u > 0), h:h + nh],
                                          max_ps[n % 2][:, :].rearrange("p (h k) -> p h k", h=nh),
                                          AX.X, ALU.max).then_inc(s["max_red"], 1)
                elif name == "maxrow" and b == 0:
                    dve.wait_ge(s["w_ex_hi"], 1)
                    dve.tensor_tensor(w_ex_lo[:, :, :, :], w_ex[:, :, :, :], w_ex_hi[:, :, :, :].bitcast(F32),
                                      ALU.subtract).then_inc(s["w_ex_lo"], 1)
                elif name == "maxrow" and b == 1:
                    dve.wait_ge(s["w_ffn_hi"], 2)
                    for w, hi, lo in ((w_up, w_up_hi, w_up_lo), (w_gx, w_gx_hi, w_gx_lo)):
                        dve.tensor_tensor(lo[:, :, :], w[:, :, :], hi[:, :, :].bitcast(F32),
                                          ALU.subtract).then_inc(s["w_ffn_lo"], 1)
                elif name == "heads":
                    n = NT * b + i
                    ps, read, _ = shared_of(step)
                    view = ps[:, :].rearrange("p (r g v) -> p r g v", r=R, g=G)
                    dve.wait_ge(s["heads_mm"], n + 1)
                    dve.reciprocal(rden[:, i, :, :], view[:, :, :, HD]).then_inc(s["rden_done"], 1)
                    dve.wait_ge(s["rden_done"], n + 1)
                    if b:
                        dve.wait_ge(s["attn_mm"], n - NT + 1)
                    dve.tensor_tensor(attn[:, i, :].rearrange("p (g r d) -> p r g d", r=R, g=G),
                                      view[:, :, :, 0:HD],
                                      rden[:, i, :, :].unsqueeze(3).to_broadcast([P, R, G, HD]),
                                      ALU.mult).then_inc(read, 1)
                elif name == "wo":
                    n = NT * b + i
                    ps, read, value = shared_of(step)
                    dve.wait_ge(s["wo_mm"], n + 1)
                    dve.wait_ge(s["x_bo_done"], b + 1)
                    dve.tensor_tensor(z[:, i, :], ps[:, 0:D], x_bo[:, n, :], ALU.add).then_inc(read, 1)
                    dve.wait_ge(read, value)
                    if b:
                        dve.wait_ge(s["x1t_mm"], n - NT + 1)
                    norms += 1
                    layernorm(norms, i, x1[:, i, :], s["x1_done"])
                elif name in ("x1t", "x2t"):
                    ps, read, _ = shared_of(step)
                    hi, lo = (x1t_hi, x1t_lo) if name == "x1t" else (x2t_hi, x2t_lo)
                    dve.wait_ge(s[name + "_hi_done"], NT * b + i + 1)
                    dve.tensor_tensor(lo[:, :, i * P:(i + 1) * P], ps[:, 0:D].rearrange("p (k q) -> p k q", k=ND),
                                      hi[:, :, i * P:(i + 1) * P].bitcast(F32), ALU.subtract).then_inc(read, 1)
                elif name == "expert":
                    n = E * b + i
                    dve.wait_ge(s["tanh_done"], n + 1)
                    dve.wait_ge(s["sqr_done"], n + 1)
                    if n >= 2:
                        dve.wait_ge(s["down_mm"], n - 1)
                    dve.scalar_tensor_tensor(out=hid[:, n % 2, :, :].rearrange("p k q -> p (k q)"),
                                             in0=th[:, n % 2, :, :].rearrange("p k q -> p (k q)"), scalar=1.0,
                                             in1=sq[:, n % 2, :, :].rearrange("p k q -> p (k q)"),
                                             op0=ALU.add, op1=ALU.mult).then_inc(s["hid_done"], 1)
                elif name == "down" and i == E - 1:
                    dve.wait_ge(s["down_mm"], E * (b + 1))
                    dve.wait_ge(s["x1_done"], NT * (b + 1))
                    for t in range(NT):
                        n = NT * b + t
                        dve.tensor_tensor(z[:, t, :], acc_ps[t][:, 0:D], x1[:, t, :], ALU.add)\
                           .then_inc(s["z2_done"], 1)
                        dve.wait_ge(s["z2_done"], n + 1)
                        if b:
                            dve.wait_ge(s["x2t_mm"], n - NT + 1)
                            dve.wait_ge(s["moe_x_done"], n - NT + 1)
                        norms += 1
                        layernorm(norms, t, x2[:, t, :], s["x2_done"])
                elif name == "gate":
                    n = NT * b + i
                    ps, read, _ = shared_of(step)
                    j = slice(i, i + 1)
                    dve.wait_ge(s["gx_mm"], n + 1)
                    dve.max(top[:, i, :], ps[:, D:D + NG]).then_inc(s["top_done"], 1)
                    dve.wait_ge(s["top_done"], n + 1)
                    dve.tensor_tensor(gd[:, j], top[:, i, 1:2], top[:, i, 0:1], ALU.subtract)\
                       .then_inc(s["gdiff_done"], 1)
                    dve.wait_ge(s["gexp_done"], n + 1)
                    dve.tensor_scalar(gs[:, j], ge[:, j], 1.0, None, ALU.add).then_inc(s["gsum_done"], 1)
                    dve.wait_ge(s["gsum_done"], n + 1)
                    dve.reciprocal(gr[:, j], gs[:, j]).then_inc(s["grec_done"], 1)
                    dve.wait_ge(s["grec_done"], n + 1)
                    if b:
                        wait_shared(dve, ("gate", b - 1, i))
                    dve.scalar_tensor_tensor(out=gw[:, j], in0=ge[:, j], scalar=gr[:, j], in1=gr[:, j],
                                             op0=ALU.mult, op1=ALU.add).then_inc(s["gw_done"], 1)
                elif name == "ffn":
                    n = NT * b + i
                    ps, read, value = shared_of(step)
                    dve.wait_ge(s["ffn_mm"], n + 1)
                    dve.wait_ge(s["moe_x_done"], n + 1)
                    dve.tensor_tensor(z[:, i, :], ps[:, 0:D], moe_x[:, i, :], ALU.add).then_inc(read, 1)
                    dve.wait_ge(read, value)
                    if b >= 2:
                        dve.wait_ge(stored[c], 16 * NT * (b // 2))
                    norms += 1
                    layernorm(norms, i, y_out[:, c, i, :], s["y_done"])

        @block.gpsimd
        def _(pool):
            norms = 0

            def power(n, i):
                pool.wait_ge(s["mv_done"], n)
                pool.tensor_scalar(veps[:, i:i + 1], mv[:, i, 1:2], EPS, None, ALU.add).then_inc(s["veps_done"], 1)
                pool.wait_ge(s["veps_done"], n)
                pool.tensor_tensor(rstd[:, i:i + 1], veps[:, i:i + 1], half_power[:, i:i + 1], ALU.pow)\
                    .then_inc(s["rstd_done"], 1)

            for step in steps():
                name, b, i = step
                c = b % 2
                if name == "project":
                    if i == 0:
                        pool.wait_ge(ld_xt[b], 16)
                        if b >= 2:
                            pool.wait_ge(s["proj_mm"], 3 * (b - 1))
                        pool.tensor_copy(xt_hi[:, :, c, :], xt[:, :, b, :]).then_inc(s["xt_hi"], 1)
                    if i < 3:
                        n = 3 * b + i
                        rows = slice(0, P if i < NQB else KVW)
                        pool.wait_ge(s["rope_cos"], n + 1)
                        wait_shared(pool, step)
                        if b:
                            pool.wait_ge(qk_moved[1 - c], NDMA_QK * ((b - 1) // 2 + 1))
                        x, rest = qk_rot[rows, i, :], qk_rest[rows, i, :]
                        hi, mid, lo = (qk_parts[rows, i, k, :] for k in range(3))
                        pool.tensor_tensor(x, rc[rows, n % 2, :], rs[rows, n % 2, :], ALU.add)\
                            .then_inc(s["rot_done"], 1)
                        pool.wait_ge(s["rot_done"], n + 1)
                        pool.tensor_copy(hi, x).then_inc(s["hi_part"], 1)
                        pool.wait_ge(s["hi_part"], n + 1)
                        pool.tensor_tensor(rest, x, hi, ALU.subtract).then_inc(s["rest_done"], 1)
                        pool.wait_ge(s["rest_done"], n + 1)
                        pool.tensor_copy(mid, rest).then_inc(s["mid_part"], 1)
                        pool.wait_ge(s["mid_part"], n + 1)
                        pool.tensor_tensor(lo, rest, mid, ALU.subtract).then_inc(s["parts_done"], 1)
                elif name == "maxrow":
                    pool.wait_ge(ld["x"], 32)
                    for t in range(NT):
                        last = pool.tensor_tensor(x_bo[:, NT * b + t, :], x_bo[:, NT * b + t, :], bo_all[:, :],
                                                  ALU.add)
                    last.then_inc(s["x_bo_done"], 1)
                    if b == 0:
                        pool.wait_ge(ld["w_ex"], 16)
                        pool.tensor_copy(w_ex_hi[:, :, :, :], w_ex[:, :, :, :]).then_inc(s["w_ex_hi"], 1)
                        pool.wait_ge(ld["tok"], 16)
                        pool.tensor_scalar(route[:, 0, :], tok[:, :], float(TPE), 0.5, ALU.is_lt, ALU.mult)\
                            .then_inc(s["route_ge"], 1)
                        for e in range(1, E):
                            pool.tensor_scalar(route[:, e, :], tok[:, :], float(e * TPE), 0.5, ALU.is_ge,
                                               ALU.mult).then_inc(s["route_ge"], 1)
                        pool.wait_ge(s["route_ge"], E)
                        for e in range(1, E - 1):
                            pool.tensor_tensor(route[:, e, :], route[:, e, :], route[:, e + 1, :],
                                               ALU.subtract).then_inc(s["route_done"], 1)
                            pool.wait_ge(s["route_done"], e)
                    elif b == 1:
                        pool.wait_ge(ld["w_ffn"], 48)
                        for w, hi in ((w_up, w_up_hi), (w_gx, w_gx_hi)):
                            pool.tensor_copy(hi[:, :, :], w[:, :, :]).then_inc(s["w_ffn_hi"], 1)
                elif name == "probs":
                    for u in (0, 2):
                        n = UNITS * (G * b + i) + u
                        pool.wait_ge(s["exp_done"], n + 1)
                        block_p = probs[:, n % (2 * UNITS), :].rearrange("p (h q) -> p h q", h=R)
                        pool.affine_select(out=block_p, in_=block_p, compare_op=ALU.is_ge, fill=0.0, base=0,
                                           pattern=[[0, R], [1, P]], channel_multiplier=-1)\
                            .then_inc(s["masked_done"], 1)
                elif name == "wo":
                    norms += 1
                    power(norms, i)
                elif name == "expert":
                    n = E * b + i
                    wait_shared(pool, step)
                    for k in range(ND):
                        last = pool.tensor_tensor(sq[:, n % 2, k, :], sq[:, n % 2, k, :],
                                                  route[:, i, b * S:(b + 1) * S], ALU.mult)
                    last.then_inc(s["sqr_done"], 1)
                elif name == "down" and i == E - 1:
                    for t in range(NT):
                        norms += 1
                        power(norms, t)
                elif name == "gate":
                    n = NT * b + i
                    wait_shared(pool, step)
                    pool.wait_ge(s["x2_done"], n + 1)
                    if b:
                        wait_shared(pool, ("ffn", b - 1, i))
                    pool.tensor_tensor(moe_x[:, i, :], moe[:, i, :], x2[:, i, :], ALU.add)\
                        .then_inc(s["moe_x_done"], 1)
                elif name == "ffn":
                    norms += 1
                    power(norms, i)


def rope_tables():
    inv = (1.0 / np.float32(1000000.0) ** (np.arange(0, HD, 2, dtype=np.float32) / np.float32(HD))).astype(np.float32)
    ang = np.arange(S, dtype=np.float32)[None, :] * inv[:, None]
    cos = np.concatenate([np.cos(ang), np.cos(ang)]).astype(np.float32)
    sin = np.concatenate([-np.sin(ang), np.sin(ang)]).astype(np.float32)
    k = np.concatenate([np.repeat(cos, G, 0), np.repeat(sin, G, 0)])
    return np.repeat(cos, HB, 0), np.repeat(sin, HB, 0), k


def by_dim(w, heads):
    w = w.reshape(w.shape[0], heads, HD)
    both = w, np.concatenate([w[:, :, HD // 2:], w[:, :, :HD // 2]], -1)
    return [v.transpose(0, 2, 1).reshape(w.shape[0], -1) for v in both]


def qk_columns(wq, wk):
    blocks = []
    for i in range(NQB):
        blocks += by_dim(wq[:, i * P:(i + 1) * P], HB)
    return np.concatenate(blocks + by_dim(wk, G), 1)


def kernel(x, itok_BxS_13_99985, ctx_2048, L0_attn_Wq, L0_attn_bq, L0_attn_Wk, L0_attn_bk, L0_attn_Wv,
           L0_attn_bv, L0_attn_Wo, L0_attn_bo, L0_ffn_W_up, L0_ffn_W_down, L0_ffn_W_gate, L0_ffn_W_expert):
    import ml_dtypes
    import concourse.bacc as bacc
    from concourse.bass_utils import run_bass_kernel_spmd as run

    x, tok, ctx = (np.asarray(v) for v in (x, itok_BxS_13_99985, ctx_2048))
    wq, bq, wk, bk, wv, bv, wo, bo = (np.asarray(v) for v in (
        L0_attn_Wq, L0_attn_bq, L0_attn_Wk, L0_attn_bk, L0_attn_Wv, L0_attn_bv, L0_attn_Wo, L0_attn_bo))
    w_up, w_dn, w_gate, w_exp = (np.asarray(v) for v in (
        L0_ffn_W_up, L0_ffn_W_down, L0_ffn_W_gate, L0_ffn_W_expert))
    cos, sin, rope_k = rope_tables()
    mask = np.where(np.arange(P)[None, :] > np.arange(P)[:, None], MASK, 0.0)
    arrays = {
        "x": x.reshape(B * S, D),
        "x_t": x.reshape(B * S, D).T,
        "tok": tok,
        "w_qk": qk_columns(wq, wk),
        "b_qk": qk_columns(bq[None], bk[None]).reshape(5, P).T,
        "w_v": wv, "b_v": bv, "w_o": wo, "b_o": bo,
        "w_ex": ctx.transpose(2, 0, 1).reshape(D, E * D),
        "w_up": w_up.T,
        "w_gx": np.concatenate([w_exp, w_gate.T], 1),
        "w_dn": w_dn.T,
        "cos": cos, "sin": sin, "rope_k": rope_k,
        "ident": np.eye(P, dtype=np.float32),
        "ident_bf": np.eye(P, dtype=np.float32).astype(ml_dtypes.bfloat16),
        "causal": np.tile(mask, (1, R)).astype(ml_dtypes.bfloat16),
    }
    arrays = {"in_" + k: np.ascontiguousarray(v) for k, v in arrays.items()}
    nc = bacc.Bacc("TRN2", target_bir_lowering=False, num_devices=1)
    a = {k[3:]: nc.dram_tensor(k, v.shape, mybir.dt.from_np(v.dtype), kind="ExternalInput").ap()
         for k, v in arrays.items()}
    a["out"] = nc.dram_tensor("out", (B * S, D), F32, kind="ExternalOutput").ap()
    decoder_layer(nc, a)
    r = run(nc, [arrays], core_ids=[0])
    return r.results[0]["out"].reshape(B, S, D)
```

```python
from contextlib import ExitStack

import numpy as np

import concourse.bass as bass
from concourse import mybir

F32 = mybir.dt.float32
F32R = mybir.dt.float32r
BF16 = mybir.dt.bfloat16
I32 = mybir.dt.int32
ALU = mybir.AluOpType
ACT = mybir.ActivationFunctionType
AX = mybir.AxisListType

P = 128
B, S, D = 4, 256, 256
NT = S // P
ND = D // P
H, G = 16, 4
R = H // G
HD = D // H
KVW = G * HD
E = 4
VOCAB = 12500
TPE = VOCAB // E
NG = 8
EPS = 1e-5
MASK = -4.0e9
SCALE = float(HD) ** -0.5
QPARTS = (0, 0, 0, 1, 1, 2)
KPARTS = (0, 1, 2, 0, 1, 0)
NPART = len(QPARTS)
KQ = NPART * HD
HB = P // HD
NQB = H // HB
UNITS = 3
VW = 2 * HD


def steps():
    yield "xsplit", 0, 0
    for b in (0, 1):
        yield from (("project", b, 0), ("project", b, 1), ("split", b, 0), ("project", b, 2),
                    ("split", b, 1), ("low", b, 0), ("xsplit", b + 1, 0), ("split", b, 2), ("low", b, 1),
                    ("project", b, 3), ("low", b, 2))
    yield from (("max", 0, u) for u in range(UNITS * G))
    yield "maxrow", 0, 0
    for b in range(B + 2):
        o, p, m, n = b - 2, b - 1, b + 1, b + 2
        between = (
            (("heads", p, 0), ("project", n, 0), ("heads", p, 1)),
            (("x2t", o, 0), ("project", n, 1), ("split", n, 0), ("x2t", o, 1)),
            (("attnt", p, 0), ("attnt", p, 1), ("low", n, 0), ("split", n, 1), ("up", o, 0)),
            (("wo", p, 0), ("wo", p, 1), ("low", n, 1)),
            (("gate", o, 0), ("norm1", p, 0), ("norm1", p, 1), ("gate", o, 1)),
            (("x1t", p, 0), ("mix", o, 0), ("x1t", p, 1), ("mix", o, 1), ("project", n, 2)),
            (("expert", p, 0), ("ffn", o, 0)),
            (("expert", p, 1), ("ffn", o, 1), ("split", n, 2)),
            (("down", p, 0), ("norm3", o, 0), ("expert", p, 2)),
            (("down", p, 1), ("norm3", o, 1)),
            (("expert", p, 3), ("down", p, 2)),
            (("down", p, 3), ("xsplit", n + 1, 0)))
        for u, follow in enumerate(between):
            for s in (("probs", b, u), ("max", m, u), *follow):
                if 0 <= s[1] < B:
                    yield s
        for s in (("maxrow", m, 0), ("pv", b, 0), ("pv", b, 1), ("low", n, 2), ("project", n, 3),
                  ("norm2", p, 0), ("norm2", p, 1)):
            if 0 <= s[1] < B:
                yield s


SHARED = 3
SHARED_USES = {"project": 1, "maxrow": 1, "pv": 1, "heads": 1, "attnt": 1, "wo": 1, "x1t": 1, "expert": 1, "x2t": 1,
               "up": 1, "gate": 1, "ffn": 1}


def shared_use():
    n, first = 0, {}
    for s in steps():
        first[s] = n
        n += SHARED_USES.get(s[0], 0)
    return first


def decoder_layer(nc, a):
    first_use = shared_use()
    with ExitStack() as ctx:
        def sb(name, shape, dt=F32):
            return ctx.enter_context(nc.sbuf_tensor(name, shape, dt))

        def bank(name, shape):
            return ctx.enter_context(nc.psum_tensor(name, shape, F32))

        def sem(name):
            return ctx.enter_context(nc.semaphore(name))

        ident = sb("ident", [P, P])
        ident_bf = sb("ident_bf", [P, P], BF16)
        causal = sb("causal", [P, R, P], BF16)
        cos, sin = sb("cos", [P, S]), sb("sin", [P, S])
        rope_k = sb("rope_k", [P, S])
        w_qk = sb("w_qk", [P, ND, 5 * P])
        w_qk_hi, w_qk_lo = sb("w_qk_hi", [P, ND, 5 * P], F32R), sb("w_qk_lo", [P, ND, 5 * P], F32R)
        b_qk = sb("b_qk", [P, 5])
        w_v = sb("w_v", [P, ND, KVW])
        bv_all = sb("bv_all", [P, NT, KVW])
        w_o = sb("w_o", [P, ND, D])
        bo_all = sb("bo_all", [P, D])
        w_ex = sb("w_ex", [P, ND, E, D])
        w_ex_hi, w_ex_lo = sb("w_ex_hi", [P, ND, E, D], F32R), sb("w_ex_lo", [P, ND, E, D], F32R)
        w_up = sb("w_up", [P, ND, D])
        w_up_hi, w_up_lo = sb("w_up_hi", [P, ND, D], F32R), sb("w_up_lo", [P, ND, D], F32R)
        w_gx = sb("w_gx", [P, ND, D + NG])
        w_gx_hi, w_gx_lo = sb("w_gx_hi", [P, ND, D + NG], F32R), sb("w_gx_lo", [P, ND, D + NG], F32R)
        w_dn = sb("w_dn", [P, ND, D])
        half_power = sb("half_power", [P, NT])
        tok = sb("tok", [P, B * S], I32)
        route = sb("route", [P, E, B * S], BF16)
        x_bo = sb("x_bo", [P, B * NT, D])
        xt = sb("xt", [P, ND, 2, S])
        xt_hi, xt_lo = sb("xt_hi", [P, ND, 2, S], F32R), sb("xt_lo", [P, ND, 2, S], F32R)
        rc, rs = sb("rc", [P, 2, S]), sb("rs", [P, 2, S])
        qk_rot, qk_rest = sb("qk_rot", [P, 3, S]), sb("qk_rest", [P, 3, S])
        qk_parts = sb("qk_parts", [P, 3, 3, S], BF16)
        q_st = sb("q_st", [KQ + 1, 2, H, S], BF16)
        k_st = sb("k_st", [KQ + 1, 3, G, S], BF16)
        v_st = sb("v_st", [P, 2, NT, G, VW])
        mx = sb("mx", [P, 2, NT, H])
        neg_mx = sb("neg_mx", [H, 2, S], BF16)
        probs = sb("probs", [P, UNITS * G, R * P])
        heads_t = sb("heads_t", [P, NT, R * P])
        rden = sb("rden", [P, NT, R, G])
        attn = sb("attn", [P, NT, D])
        attn_t = sb("attn_t", [P, NT, ND, P])
        z = sb("z", [P, 3, NT, D])
        stats = sb("stats", [P, 3, NT, 6])
        mv = sb("mv", [P, 3, NT, 2])
        veps, rstd = sb("veps", [P, 3, NT]), sb("rstd", [P, 3, NT])
        x1, x2 = sb("x1", [P, NT, D]), sb("x2", [P, NT, D])
        x1t_hi, x1t_lo = sb("x1t_hi", [P, ND, S], F32R), sb("x1t_lo", [P, ND, S], F32R)
        x2t_hi, x2t_lo = sb("x2t_hi", [P, ND, S], F32R), sb("x2t_lo", [P, ND, S], F32R)
        th, sq = sb("th", [P, 2, ND, S]), sb("sq", [P, 2, ND, S])
        hid = sb("hid", [P, 2, ND, S])
        up_t = sb("up_t", [P, ND, S])
        top = sb("top", [P, NT, 8])
        gd, ge, gs, gr, gw, gt = (sb(n, [P, NT]) for n in ("gd", "ge", "gs", "gr", "gw", "gt"))
        moe, moe_x = sb("moe", [P, NT, D]), sb("moe_x", [P, NT, D])
        y_out = sb("y_out", [P, 2, NT, D])

        max_ps = [bank(f"max_ps{i}", [P, 512]) for i in range(2)]
        sc_ps = [bank(f"sc_ps{i}", [P, 512]) for i in range(2)]
        down_ps = bank("down_ps", [P, NT, D])
        shared = [bank(f"shared{i}", [P, 512]) for i in range(SHARED)]

        ld = {n: sem("ld_" + n) for n in ("w_k", "w_q", "tabs", "w_v", "mask", "tok", "w_o", "w_ex", "w_ffn", "x")}
        ld_xt = [sem(f"ld_xt{b}") for b in range(B)]
        names = ("w_qk_hi w_qk_lo xt_hi xt_lo w_ex_hi w_ex_lo w_ffn_hi w_ffn_lo consts pool_consts route_ge route_mid "
                 "route_done x_bo_done proj_mm v_mm rope_cos rope_sin rot_done hi_part rest_done mid_part parts_done "
                 "max_mm max_red mxt_mm score_mm exp_done masked_done pv_mm heads_mm "
                 "rden_done attn_mm wo_mm x1_done x1t_mm x1t_hi_done "
                 "gate_mm tanh_done sqr_done hid_done down_mm  x2_done x2t_mm x2t_hi_done up_mm "
                 "gx_mm top_done gdiff_done gexp_done gsum_done grec_done gw_done moe_x_done ffn_mm "
                 "y_done").split()
        s = {n: sem(n) for n in names}
        z_done, stats_done, mv_done, veps_done, rstd_done = (
            [sem(f"{n}{k}") for k in range(3)] for n in ("z_done", "stats_done", "mv_done", "veps_done", "rstd_done"))
        moved = [sem(f"moved{i}") for i in range(3)]
        mx_moved = [sem(f"mx_moved{i}") for i in range(2)]
        stored = [sem(f"stored{i}") for i in range(2)]
        shared_read = [sem(f"shared_read{i}") for i in range(SHARED)]

        MOVED = 16 * NPART

        def take_shared(pe, step, k=0):
            n = first_use[step] + k
            if n >= SHARED:
                pe.wait_ge(shared_read[n % SHARED], n // SHARED)
            return shared[n % SHARED]

        def shared_of(step, k=0):
            n = first_use[step] + k
            return shared[n % SHARED], shared_read[n % SHARED], n // SHARED + 1

        def wait_shared(eng, step, k=0):
            _, read, value = shared_of(step, k)
            eng.wait_ge(read, value)

        def three_pass(pe, out, w_hi, w_lo, m_hi, m_lo):
            n = len(w_hi)
            for k in range(n):
                pe.matmul(out, w_hi[k], m_hi[k], start=(k == 0), stop=False)
                pe.matmul(out, w_hi[k], m_lo[k], start=False, stop=False)
                last = pe.matmul(out, w_lo[k], m_hi[k], start=False, stop=(k == n - 1))
            return last

        block = ctx.enter_context(nc.Block())

        @block.sync
        def _(sp):
            def load(dst, src, signal):
                sp.dma_start(dst, src).then_inc(signal, 16)

            w_qk_view = a["w_qk"].rearrange("(k p) n -> p k n", p=P)
            load(w_qk[:, :, 0:P], w_qk_view[:, :, 0:P], ld["w_k"])
            xt_view = a["x_t"].rearrange("(k p) (b s) -> p k b s", p=P, b=B)
            load(xt[:, :, 0, :], xt_view[:, :, 0, :], ld_xt[0])
            load(w_qk[:, :, P:5 * P], w_qk_view[:, :, P:5 * P], ld["w_q"])
            load(cos[:, :], a["cos"], ld["tabs"])
            load(sin[:, :], a["sin"], ld["tabs"])
            load(rope_k[:, :], a["rope_k"], ld["tabs"])
            load(b_qk[:, :], a["b_qk"], ld["tabs"])
            load(w_v[:, :, :], a["w_v"].rearrange("(k p) n -> p k n", p=P), ld["w_v"])
            load(bv_all[:, :, :], a["b_v"].rearrange("(o t n) -> o t n", o=1, t=1).to_broadcast([P, NT, KVW]),
                 ld["w_v"])
            load(xt[:, :, 1, :], xt_view[:, :, 1, :], ld_xt[1])
            load(causal[:, :, :], a["causal"].rearrange("p (r k) -> p r k", r=R), ld["mask"])
            load(ident_bf[:, :], a["ident_bf"], ld["mask"])
            load(ident[:, :], a["ident"], ld["mask"])
            load(tok[:, :], a["tok"].rearrange("b s -> (b s)").rearrange("(o n) -> o n", o=1)
                 .to_broadcast([P, B * S]), ld["tok"])
            load(w_ex[:, :, :, :], a["w_ex"].rearrange("(k p) (e f) -> p k e f", p=P, e=E), ld["w_ex"])
            load(x_bo[:, :, :], a["x"].rearrange("(t p) d -> p t d", p=P), ld["x"])
            load(bo_all[:, :], a["b_o"].rearrange("(o n) -> o n", o=1).to_broadcast([P, D]), ld["x"])
            load(w_o[:, :, :], a["w_o"].rearrange("(k p) n -> p k n", p=P), ld["w_o"])
            load(w_up[:, :, :], a["w_up"].rearrange("(k p) n -> p k n", p=P), ld["w_ffn"])
            load(w_gx[:, :, :], a["w_gx"].rearrange("(k p) n -> p k n", p=P), ld["w_ffn"])
            load(w_dn[:, :, :], a["w_dn"].rearrange("(k p) n -> p k n", p=P), ld["w_ffn"])

            for step in steps():
                name, b, i = step
                c = b % 2
                if name == "project" and i == 3 and b + 2 < B:
                    sp.wait_ge(s["v_mm"], b + 1)
                    sp.wait_ge(s["xt_lo"], b + 1)
                    load(xt[:, :, c, :], xt_view[:, :, b + 2, :], ld_xt[b + 2])
                elif name == "low":
                    sp.wait_ge(s["parts_done"], 3 * b + i + 1)
                    read = (UNITS * G * (b - 2), UNITS * G * (b - 2) + UNITS * G // 2, UNITS * G * (b - 1))[i]
                    if b >= (3, 2, 2)[i]:
                        sp.wait_ge(s["score_mm"], read)
                    for n in range(NPART):
                        rows = slice(n * HD, (n + 1) * HD)
                        if i:
                            dst = q_st[rows, c, HB * (i - 1):HB * i, :]
                            src = qk_parts[:, i, QPARTS[n], :]
                        else:
                            dst = k_st[rows, b % 3, :, :]
                            src = qk_parts[0:KVW, i, KPARTS[n], :]
                        sp.dma_start(dst, src).then_inc(moved[i], 16)
                elif name == "maxrow":
                    wait_shared(sp, step)
                    sp.dma_start(q_st[KQ:KQ + 1, c, :, :], neg_mx[:, c, :]).then_inc(mx_moved[c], 16)
                elif name == "norm3":
                    sp.wait_ge(s["y_done"], NT * b + i + 1)
                    t = NT * b + i
                    sp.dma_start(a["out"][t * P:(t + 1) * P, :], y_out[:, c, i, :]).then_inc(stored[c], 16)
            sp.wait_ge(stored[0], 16 * NT * 2)
            sp.wait_ge(stored[1], 16 * NT * 2)

        @block.tensor
        def _(pe):
            for step in steps():
                name, b, i = step
                c = b % 2
                if name == "project":
                    ps = take_shared(pe, step)
                    if i < 3:
                        pe.wait_ge(s["w_qk_lo"], 1 if i == 0 else 2)
                        pe.wait_ge(s["xt_lo"], b + 1)
                        for n in range(2 if i else 1):
                            col = max(2 * i - 1, 0) + n
                            cols = slice(col * P, (col + 1) * P)
                            last = three_pass(pe, ps[:, n * S:(n + 1) * S],
                                              [w_qk_hi[:, k, cols] for k in range(ND)],
                                              [w_qk_lo[:, k, cols] for k in range(ND)],
                                              [xt_hi[:, k, c, :] for k in range(ND)],
                                              [xt_lo[:, k, c, :] for k in range(ND)])
                        last.then_inc(s["proj_mm"], 1)
                    else:
                        pe.wait_ge(ld["w_v"], 32)
                        pe.wait_ge(ld_xt[b], 16)
                        for t in range(NT):
                            for k in range(ND):
                                last = pe.matmul(ps[:, t * KVW:(t + 1) * KVW],
                                                 xt[:, k, c, t * P:(t + 1) * P], w_v[:, k, :],
                                                 start=(k == 0), stop=(k == ND - 1))
                        last.then_inc(s["v_mm"], 1)
                elif name == "max":
                    g, u = divmod(i, UNITS)
                    if i == 0:
                        pe.wait_ge(moved[0], MOVED * (b + 1))
                        pe.wait_ge(moved[1], MOVED * (b + 1))
                        pe.wait_ge(ld["mask"], 48)
                    if i == UNITS * G // 2:
                        pe.wait_ge(moved[2], MOVED * (b + 1))
                    n = UNITS * G * b + i
                    if n >= 2:
                        pe.wait_ge(s["max_red"], n - 1)
                    ps = max_ps[n % 2]
                    if u == 0:
                        out = ps[:, :].rearrange("p (h k) -> p h k", h=R)
                        pe.matmul(out, ident_bf[:, :], causal[:, :, :], start=True, stop=False,
                                  skip_group_check=True)
                        hs, q0, nk = range(R), 0, P
                    else:
                        out = ps[:, :].rearrange("p (h k) -> p h k", h=2)
                        pe.matmul(out[:, :, P:S], ident_bf[:, :], causal[:, 0:2, :],
                                  start=True, stop=False, skip_group_check=True)
                        hs, q0, nk = range(2 * (u - 1), 2 * u), P, S
                    for m, h in enumerate(hs):
                        last = pe.matmul(out[:, m, :], q_st[0:KQ, c, R * g + h, q0:q0 + P],
                                         k_st[0:KQ, b % 3, g, 0:nk], start=False, stop=(h == hs[-1]),
                                         skip_group_check=True)
                    last.then_inc(s["max_mm"], 1)
                elif name == "maxrow":
                    ps = take_shared(pe, step)
                    pe.wait_ge(s["max_red"], UNITS * G * (b + 1))
                    for t in range(NT):
                        last = pe.transpose(ps[0:H, t * P:(t + 1) * P], mx[:, c, t, :], ident[:, :])
                    last.then_inc(s["mxt_mm"], 1)
                elif name == "probs":
                    if i == 0:
                        pe.wait_ge(mx_moved[c], 16 * (b // 2 + 1))
                        pe.wait_ge(s["pool_consts"], 1)
                    g, u = divmod(i, UNITS)
                    t, k = ((0, 0), (1, 0), (1, 1))[u]
                    n = UNITS * G * b + i
                    if n >= 2:
                        pe.wait_ge(s["exp_done"], n - 1)
                    pe.matmul(sc_ps[n % 2][:, :], k_st[:, b % 3, g, k * P:(k + 1) * P],
                              q_st[:, c, R * g:R * (g + 1), t * P:(t + 1) * P],
                              start=True, stop=True).then_inc(s["score_mm"], 1)
                elif name == "pv":
                    ps = take_shared(pe, step)
                    wait_shared(pe, ("project", b, 3))
                    pe.wait_ge(s["exp_done"], UNITS * G * (b + 1))
                    pe.wait_ge(s["masked_done"], 2 * G * (b + 1))
                    for k in range(i + 1):
                        for g in range(G):
                            last = pe.matmul(ps[32 * g:32 * g + VW, :], v_st[:, c, k, g, :],
                                             probs[:, UNITS * g + i + k, :], start=(k == 0), stop=(k == i),
                                             tile_position=(0, 32 * g))
                    last.then_inc(s["pv_mm"], 1)
                elif name == "heads":
                    ps = take_shared(pe, step)
                    wait_shared(pe, ("pv", b, i))
                    for r in range(R):
                        last = pe.transpose(ps[:, r * P:(r + 1) * P], heads_t[:, i, r * P:(r + 1) * P],
                                            ident[:, :])
                    last.then_inc(s["heads_mm"], 1)
                elif name == "attnt":
                    ps = take_shared(pe, step)
                    wait_shared(pe, ("heads", b, i))
                    for k in range(ND):
                        last = pe.transpose(ps[:, k * P:(k + 1) * P], attn[:, i, k * P:(k + 1) * P],
                                            ident[:, :])
                    last.then_inc(s["attn_mm"], 1)
                elif name == "wo":
                    ps = take_shared(pe, step)
                    wait_shared(pe, ("attnt", b, i))
                    pe.wait_ge(ld["w_o"], 16)
                    for k in range(ND):
                        last = pe.matmul(ps[:, 0:D], attn_t[:, i, k, :], w_o[:, k, :],
                                         start=(k == 0), stop=(k == ND - 1))
                    last.then_inc(s["wo_mm"], 1)
                elif name in ("x1t", "x2t"):
                    src = x1 if name == "x1t" else x2
                    ps = take_shared(pe, step)
                    pe.wait_ge(s[name[:2] + "_done"], NT * b + i + 1)
                    for k in range(ND):
                        last = pe.transpose(ps[:, k * P:(k + 1) * P], src[:, i, k * P:(k + 1) * P],
                                            ident[:, :])
                    last.then_inc(s[name + "_mm"], 1)
                elif name == "expert":
                    ps = take_shared(pe, step)
                    pe.wait_ge(s["w_ex_lo"], 1)
                    for t in range(NT):
                        wait_shared(pe, ("x1t", b, t))
                    for m in range(ND):
                        cols = slice(m * P, (m + 1) * P)
                        last = three_pass(pe, ps[:, m * S:(m + 1) * S],
                                          [w_ex_hi[:, k, i, cols] for k in range(ND)],
                                          [w_ex_lo[:, k, i, cols] for k in range(ND)],
                                          [x1t_hi[:, k, :] for k in range(ND)],
                                          [x1t_lo[:, k, :] for k in range(ND)])
                    last.then_inc(s["gate_mm"], 1)
                elif name == "down":
                    n = E * b + i
                    pe.wait_ge(s["hid_done"], n + 1)
                    if i == 0 and b:
                        pe.wait_ge(z_done[1], b)
                    for t in range(NT):
                        for k in range(ND):
                            last = pe.matmul(down_ps[:, t, :], hid[:, n % 2, k, t * P:(t + 1) * P],
                                             w_ex[:, k, i, :], start=(i == 0 and k == 0 and t == 0),
                                             stop=(i == E - 1 and k == ND - 1), skip_group_check=True)
                    last.then_inc(s["down_mm"], 1)
                elif name == "up":
                    ps = take_shared(pe, step)
                    pe.wait_ge(s["w_ffn_lo"], 2)
                    for t in range(NT):
                        wait_shared(pe, ("x2t", b, t))
                    for m in range(ND):
                        cols = slice(m * P, (m + 1) * P)
                        last = three_pass(pe, ps[:, m * S:(m + 1) * S],
                                          [w_up_hi[:, k, cols] for k in range(ND)],
                                          [w_up_lo[:, k, cols] for k in range(ND)],
                                          [x2t_hi[:, k, :] for k in range(ND)],
                                          [x2t_lo[:, k, :] for k in range(ND)])
                    last.then_inc(s["up_mm"], 1)
                elif name == "gate":
                    ps = take_shared(pe, step)
                    tt = slice(i * P, (i + 1) * P)
                    three_pass(pe, ps[:, 0:D + NG],
                               [x2t_hi[:, k, tt] for k in range(ND)], [x2t_lo[:, k, tt] for k in range(ND)],
                               [w_gx_hi[:, k, :] for k in range(ND)], [w_gx_lo[:, k, :] for k in range(ND)],
                               ).then_inc(s["gx_mm"], 1)
                elif name == "ffn":
                    ps = take_shared(pe, step)
                    wait_shared(pe, ("up", b, 0))
                    for k in range(ND):
                        last = pe.matmul(ps[:, 0:D], up_t[:, k, i * P:(i + 1) * P], w_dn[:, k, :],
                                         start=(k == 0), stop=(k == ND - 1))
                    last.then_inc(s["ffn_mm"], 1)

        @block.scalar
        def _(act):
            for n, cols in enumerate((slice(0, P), slice(P, 5 * P))):
                act.wait_ge(ld[("w_k", "w_q")[n]], 16)
                act.activation(w_qk_hi[:, :, cols], w_qk[:, :, cols], ACT.Copy).then_inc(s["w_qk_hi"], 1)

            def ffn_highs():
                act.wait_ge(ld["w_ffn"], 48)
                for w, hi in ((w_up, w_up_hi), (w_gx, w_gx_hi)):
                    act.activation(hi[:, :, :], w[:, :, :], ACT.Copy).then_inc(s["w_ffn_hi"], 1)

            def expert_highs():
                act.wait_ge(ld["w_ex"], 16)
                act.activation(w_ex_hi[:, :, :, :], w_ex[:, :, :, :], ACT.Copy).then_inc(s["w_ex_hi"], 1)

            for step in steps():
                name, b, i = step
                c = b % 2
                if name == "probs":
                    n = UNITS * G * b + i
                    act.wait_ge(s["score_mm"], n + 1)
                    if b and i == 0:
                        act.wait_ge(s["pv_mm"], NT * b)
                    act.activation(probs[:, i, :], sc_ps[n % 2][:, :], ACT.Exp, scale=SCALE)\
                       .then_inc(s["exp_done"], 1)
                elif name == "project" and i < 3:
                    act.wait_ge(s["rot_done"], 3 * b + i + 1)
                    if b:
                        act.wait_ge(moved[i], MOVED * b)
                    rows = slice(0, P if i else KVW)
                    act.activation(qk_parts[rows, i, 0, :], qk_rot[rows, i, :], ACT.Copy)\
                       .then_inc(s["hi_part"], 1)
                elif name == "split":
                    rows = slice(0, P if i else KVW)
                    act.wait_ge(s["rest_done"], 3 * b + i + 1)
                    act.activation(qk_parts[rows, i, 1, :], qk_rest[rows, i, :], ACT.Copy)\
                       .then_inc(s["mid_part"], 1)
                elif name == "maxrow":
                    ps, read, _ = shared_of(step)
                    act.wait_ge(s["mxt_mm"], b + 1)
                    if b >= 2:
                        act.wait_ge(mx_moved[c], 16 * (b // 2))
                    act.activation(neg_mx[:, c, :], ps[0:H, 0:S], ACT.Copy, scale=-1.0).then_inc(read, 1)
                    if b == 0:
                        expert_highs()
                        ffn_highs()
                elif name == "pv":
                    n = NT * b + i
                    ps, read, _ = shared_of(step)
                    act.wait_ge(s["pv_mm"], n + 1)
                    if b:
                        act.wait_ge(s["heads_mm"], n - NT + 1)
                    act.activation(heads_t[:, i, :], ps[:, :], ACT.Copy).then_inc(read, 1)
                elif name == "attnt":
                    n = NT * b + i
                    ps, read, _ = shared_of(step)
                    act.wait_ge(s["attn_mm"], n + 1)
                    if b:
                        act.wait_ge(s["wo_mm"], n - NT + 1)
                    act.activation(attn_t[:, i, :, :], ps[:, 0:D].rearrange("p (k q) -> p k q", k=ND),
                                   ACT.Copy).then_inc(read, 1)
                elif name in ("x1t", "x2t"):
                    ps, _, _ = shared_of(step)
                    act.wait_ge(s[name + "_mm"], NT * b + i + 1)
                    if b and name == "x1t":
                        act.wait_ge(s["gate_mm"], E * b)
                    if b and name == "x2t":
                        act.wait_ge(s["gx_mm"], NT * b)
                    hi = x1t_hi if name == "x1t" else x2t_hi
                    act.activation(hi[:, :, i * P:(i + 1) * P], ps[:, 0:D].rearrange("p (k q) -> p k q", k=ND),
                                   ACT.Copy).then_inc(s[name + "_hi_done"], 1)
                elif name == "expert":
                    n = E * b + i
                    ps, read, _ = shared_of(step)
                    act.wait_ge(s["gate_mm"], n + 1)
                    if n >= 2:
                        act.wait_ge(s["hid_done"], n - 1)
                    g = ps[:, :].rearrange("p (m q) -> p m q", m=ND)
                    act.activation(th[:, n % 2, :, :], g, ACT.Tanh, scale=0.5).then_inc(s["tanh_done"], 1)
                    act.activation(sq[:, n % 2, :, :], g, ACT.Square).then_inc(read, 1)
                elif name == "up":
                    ps, read, _ = shared_of(step)
                    act.wait_ge(s["up_mm"], b + 1)
                    if b:
                        act.wait_ge(s["ffn_mm"], NT * b)
                    act.activation(up_t[:, :, :], ps[:, :].rearrange("p (m q) -> p m q", m=ND),
                                   ACT.Relu).then_inc(read, 1)
                elif name == "gate":
                    n = NT * b + i
                    act.wait_ge(s["gdiff_done"], n + 1)
                    if b:
                        act.wait_ge(s["gw_done"], n - NT + 1)
                    act.activation(ge[:, i:i + 1], gd[:, i:i + 1], ACT.Exp).then_inc(s["gexp_done"], 1)
                elif name == "mix":
                    n = NT * b + i
                    ps, read, _ = shared_of(("gate", b, i))
                    act.wait_ge(s["gw_done"], n + 1)
                    if b:
                        act.wait_ge(s["moe_x_done"], n - NT + 1)
                    act.activation(moe[:, i, :], ps[:, 0:D], ACT.Copy, scale=gw[:, i:i + 1]).then_inc(read, 1)

        @block.vector
        def _(dve):
            dve.memset(v_st[:, :, :, :, :], 1.0).then_inc(s["consts"], 1)

            def moments(k, b, t):
                n = NT * b + t + 1
                dve.bn_stats(stats[:, k, t, :], z[:, k, t, :]).then_inc(stats_done[k], 1)
                dve.wait_ge(stats_done[k], n)
                if b:
                    dve.wait_ge(rstd_done[k], n - NT)
                dve.bn_aggr(mv[:, k, t, :], stats[:, k, t, :]).then_inc(mv_done[k], 1)

            def normalise(k, b, t, out, signal):
                dve.wait_ge(rstd_done[k], NT * b + t + 1)
                dve.tensor_scalar(out, z[:, k, t, :], mv[:, k, t, 0:1], rstd[:, k, t:t + 1],
                                  ALU.subtract, ALU.mult).then_inc(signal, 1)

            for step in steps():
                name, b, i = step
                c = b % 2
                if name == "xsplit":
                    dve.wait_ge(ld_xt[b], 16)
                    if b >= 2:
                        dve.wait_ge(s["proj_mm"], 3 * (b - 1))
                    dve.tensor_copy(xt_hi[:, :, c, :], xt[:, :, c, :]).then_inc(s["xt_hi"], 1)
                    dve.wait_ge(s["xt_hi"], b + 1)
                    dve.tensor_tensor(xt_lo[:, :, c, :], xt[:, :, c, :], xt_hi[:, :, c, :].bitcast(F32),
                                      ALU.subtract).then_inc(s["xt_lo"], 1)
                    if b == 0:
                        for n, cols in enumerate((slice(0, P), slice(P, 5 * P))):
                            dve.wait_ge(s["w_qk_hi"], n + 1)
                            dve.tensor_tensor(w_qk_lo[:, :, cols], w_qk[:, :, cols],
                                              w_qk_hi[:, :, cols].bitcast(F32), ALU.subtract)\
                               .then_inc(s["w_qk_lo"], 1)
                elif name == "project":
                    ps, read, _ = shared_of(step)
                    if i < 3:
                        n = 3 * b + i
                        dve.wait_ge(s["proj_mm"], n + 1)
                        dve.wait_ge(ld["tabs"], 64)
                        if n >= 2:
                            dve.wait_ge(s["rot_done"], n - 1)
                        rows = slice(0, P if i else KVW)
                    if i in (1, 2):
                        dve.scalar_tensor_tensor(out=rc[:, n % 2, :], in0=ps[:, 0:S],
                                                 scalar=b_qk[:, 2 * i - 1:2 * i], in1=cos[:, :],
                                                 op0=ALU.add, op1=ALU.mult).then_inc(s["rope_cos"], 1)
                        dve.scalar_tensor_tensor(out=rs[:, n % 2, :], in0=ps[:, S:2 * S],
                                                 scalar=b_qk[:, 2 * i:2 * i + 1], in1=sin[:, :],
                                                 op0=ALU.add, op1=ALU.mult).then_inc(read, 1)
                    elif i == 0:
                        dve.scalar_tensor_tensor(out=rc[0:KVW, n % 2, :], in0=ps[0:KVW, 0:S],
                                                 scalar=b_qk[0:KVW, 0:1], in1=rope_k[0:KVW, :],
                                                 op0=ALU.add, op1=ALU.mult).then_inc(s["rope_cos"], 1)
                        dve.scalar_tensor_tensor(out=rs[0:KVW, n % 2, :], in0=ps[KVW:P, 0:S],
                                                 scalar=b_qk[KVW:P, 0:1], in1=rope_k[KVW:P, :],
                                                 op0=ALU.add, op1=ALU.mult).then_inc(read, 1)
                    if i < 3:
                        dve.wait_ge(s["rope_cos"], n + 1)
                        dve.wait_ge(shared_of(step)[1], shared_of(step)[2])
                        if b:
                            dve.wait_ge(s["rest_done"], 3 * b + i - 2)
                            dve.wait_ge(s["hi_part"], 3 * b + i - 2)
                        dve.tensor_tensor(qk_rot[rows, i, :], rc[rows, n % 2, :], rs[rows, n % 2, :],
                                          ALU.add).then_inc(s["rot_done"], 1)
                    else:
                        dve.wait_ge(s["v_mm"], b + 1)
                        dve.wait_ge(ld["w_v"], 32)
                        if b == 0:
                            dve.wait_ge(s["consts"], 1)
                        if b >= 2:
                            dve.wait_ge(s["pv_mm"], NT * (b - 1))
                        dve.tensor_tensor(v_st[:, c, :, :, 0:HD],
                                          ps[:, 0:NT * KVW].rearrange("p (t g d) -> p t g d", t=NT, g=G),
                                          bv_all[:, :, :].rearrange("p t (g d) -> p t g d", g=G),
                                          ALU.add).then_inc(read, 1)
                elif name == "split":
                    rows = slice(0, P if i else KVW)
                    dve.wait_ge(s["hi_part"], 3 * b + i + 1)
                    if b:
                        dve.wait_ge(s["parts_done"], 3 * b + i - 2)
                        dve.wait_ge(s["mid_part"], 3 * b + i - 2)
                    dve.tensor_tensor(qk_rest[rows, i, :], qk_rot[rows, i, :], qk_parts[rows, i, 0, :],
                                      ALU.subtract).then_inc(s["rest_done"], 1)
                elif name == "low":
                    rows = slice(0, P if i else KVW)
                    dve.wait_ge(s["mid_part"], 3 * b + i + 1)
                    dve.tensor_tensor(qk_parts[rows, i, 2, :], qk_rest[rows, i, :], qk_parts[rows, i, 1, :],
                                      ALU.subtract).then_inc(s["parts_done"], 1)
                elif name == "max":
                    if b >= 2 and i == 0:
                        dve.wait_ge(s["mxt_mm"], b - 1)
                    g, u = divmod(i, UNITS)
                    n = UNITS * G * b + i
                    dve.wait_ge(s["max_mm"], n + 1)
                    h, nh = (R * g, R) if u == 0 else (R * g + 2 * (u - 1), 2)
                    dve.tensor_reduce(mx[:, c, int(u > 0), h:h + nh],
                                      max_ps[n % 2][:, :].rearrange("p (h k) -> p h k", h=nh),
                                      AX.X, ALU.max).then_inc(s["max_red"], 1)
                elif name == "maxrow" and b == 0:
                    dve.wait_ge(s["w_ex_hi"], 1)
                    dve.tensor_tensor(w_ex_lo[:, :, :, :], w_ex[:, :, :, :], w_ex_hi[:, :, :, :].bitcast(F32),
                                      ALU.subtract).then_inc(s["w_ex_lo"], 1)
                    dve.wait_ge(ld["tok"], 16)
                    dve.tensor_scalar(route[:, 0, :], tok[:, :], float(TPE), 0.5, ALU.is_lt, ALU.mult)\
                       .then_inc(s["route_ge"], 1)
                    for e in range(1, E):
                        dve.tensor_scalar(route[:, e, :], tok[:, :], float(e * TPE), 0.5, ALU.is_ge,
                                          ALU.mult).then_inc(s["route_ge"], 1)
                    dve.wait_ge(s["route_ge"], E)
                    for e in range(1, E - 1):
                        dve.tensor_tensor(route[:, e, :], route[:, e, :], route[:, e + 1, :],
                                          ALU.subtract).then_inc(s["route_done"], 1)
                        dve.wait_ge(s["route_done"], e)
                elif name == "maxrow" and b == 1:
                    dve.wait_ge(s["w_ffn_hi"], 2)
                    for w, hi, lo in ((w_up, w_up_hi, w_up_lo), (w_gx, w_gx_hi, w_gx_lo)):
                        dve.tensor_tensor(lo[:, :, :], w[:, :, :], hi[:, :, :].bitcast(F32),
                                          ALU.subtract).then_inc(s["w_ffn_lo"], 1)
                elif name == "heads":
                    n = NT * b + i
                    ps, read, _ = shared_of(step)
                    view = ps[:, :].rearrange("p (r g v) -> p r g v", r=R, g=G)
                    dve.wait_ge(s["heads_mm"], n + 1)
                    dve.reciprocal(rden[:, i, :, :], view[:, :, :, HD]).then_inc(s["rden_done"], 1)
                    dve.wait_ge(s["rden_done"], n + 1)
                    if b:
                        dve.wait_ge(s["attn_mm"], n - NT + 1)
                    dve.tensor_tensor(attn[:, i, :].rearrange("p (g r d) -> p r g d", r=R, g=G),
                                      view[:, :, :, 0:HD],
                                      rden[:, i, :, :].unsqueeze(3).to_broadcast([P, R, G, HD]),
                                      ALU.mult).then_inc(read, 1)
                elif name == "wo":
                    n = NT * b + i
                    ps, read, value = shared_of(step)
                    dve.wait_ge(s["wo_mm"], n + 1)
                    dve.wait_ge(s["x_bo_done"], b + 1)
                    if b:
                        dve.wait_ge(s["x1_done"], n - NT + 1)
                    dve.tensor_tensor(z[:, 0, i, :], ps[:, 0:D], x_bo[:, n, :], ALU.add).then_inc(read, 1)
                    dve.wait_ge(read, value)
                    moments(0, b, i)
                elif name == "norm1":
                    n = NT * b + i
                    if b:
                        dve.wait_ge(s["x1t_mm"], n - NT + 1)
                        dve.wait_ge(z_done[1], b)
                    normalise(0, b, i, x1[:, i, :], s["x1_done"])
                elif name in ("x1t", "x2t"):
                    ps, read, _ = shared_of(step)
                    hi, lo = (x1t_hi, x1t_lo) if name == "x1t" else (x2t_hi, x2t_lo)
                    dve.wait_ge(s[name + "_hi_done"], NT * b + i + 1)
                    dve.tensor_tensor(lo[:, :, i * P:(i + 1) * P], ps[:, 0:D].rearrange("p (k q) -> p k q", k=ND),
                                      hi[:, :, i * P:(i + 1) * P].bitcast(F32), ALU.subtract).then_inc(read, 1)
                elif name == "expert":
                    n = E * b + i
                    dve.wait_ge(s["tanh_done"], n + 1)
                    dve.wait_ge(s["sqr_done"], n + 1)
                    if n >= 2:
                        dve.wait_ge(s["down_mm"], n - 1)
                    dve.scalar_tensor_tensor(out=hid[:, n % 2, :, :].rearrange("p k q -> p (k q)"),
                                             in0=th[:, n % 2, :, :].rearrange("p k q -> p (k q)"), scalar=1.0,
                                             in1=sq[:, n % 2, :, :].rearrange("p k q -> p (k q)"),
                                             op0=ALU.add, op1=ALU.mult).then_inc(s["hid_done"], 1)
                elif name == "down" and i == E - 1:
                    dve.wait_ge(s["down_mm"], E * (b + 1))
                    dve.wait_ge(s["x1_done"], NT * (b + 1))
                    if b:
                        dve.wait_ge(s["x2_done"], NT * b)
                    dve.tensor_tensor(z[:, 1, :, :], down_ps[:, :, :], x1[:, :, :], ALU.add).then_inc(z_done[1], 1)
                    dve.wait_ge(z_done[1], b + 1)
                    for t in range(NT):
                        moments(1, b, t)
                elif name == "norm2":
                    n = NT * b + i
                    if b:
                        dve.wait_ge(s["x2t_mm"], n - NT + 1)
                        dve.wait_ge(s["moe_x_done"], n - NT + 1)
                    normalise(1, b, i, x2[:, i, :], s["x2_done"])
                elif name == "gate":
                    n = NT * b + i
                    ps, read, _ = shared_of(step)
                    j = slice(i, i + 1)
                    dve.wait_ge(s["gx_mm"], n + 1)
                    dve.max(top[:, i, :], ps[:, D:D + NG]).then_inc(s["top_done"], 1)
                    dve.wait_ge(s["top_done"], n + 1)
                    dve.tensor_tensor(gd[:, j], top[:, i, 1:2], top[:, i, 0:1], ALU.subtract)\
                       .then_inc(s["gdiff_done"], 1)
                elif name == "mix":
                    n = NT * b + i
                    j = slice(i, i + 1)
                    dve.wait_ge(s["gexp_done"], n + 1)
                    dve.tensor_scalar(gs[:, j], ge[:, j], 1.0, None, ALU.add).then_inc(s["gsum_done"], 1)
                    dve.wait_ge(s["gsum_done"], n + 1)
                    dve.reciprocal(gr[:, j], gs[:, j]).then_inc(s["grec_done"], 1)
                    dve.wait_ge(s["grec_done"], n + 1)
                    if b:
                        wait_shared(dve, ("gate", b - 1, i))
                    dve.scalar_tensor_tensor(out=gw[:, j], in0=ge[:, j], scalar=gr[:, j], in1=gr[:, j],
                                             op0=ALU.mult, op1=ALU.add).then_inc(s["gw_done"], 1)
                elif name == "ffn":
                    n = NT * b + i
                    ps, read, value = shared_of(step)
                    dve.wait_ge(s["ffn_mm"], n + 1)
                    dve.wait_ge(s["moe_x_done"], n + 1)
                    if b:
                        dve.wait_ge(s["y_done"], n - NT + 1)
                    dve.tensor_tensor(z[:, 2, i, :], ps[:, 0:D], moe_x[:, i, :], ALU.add).then_inc(read, 1)
                    dve.wait_ge(read, value)
                    moments(2, b, i)
                elif name == "norm3":
                    if b >= 2:
                        dve.wait_ge(stored[c], 16 * NT * (b // 2))
                    normalise(2, b, i, y_out[:, c, i, :], s["y_done"])

        @block.gpsimd
        def _(pool):
            pool.memset(k_st[KQ:KQ + 1, :, :, :], 1.0).then_inc(s["pool_consts"], 1)
            pool.wait_ge(s["pool_consts"], 1)
            pool.memset(half_power[:, :], -0.5).then_inc(s["pool_consts"], 1)
            pool.wait_ge(s["pool_consts"], 2)

            def power(k, b, t):
                n = NT * b + t + 1
                pool.wait_ge(mv_done[k], n)
                pool.tensor_scalar(veps[:, k, t:t + 1], mv[:, k, t, 1:2], EPS, None, ALU.add)\
                    .then_inc(veps_done[k], 1)
                pool.wait_ge(veps_done[k], n)
                if b:
                    pool.wait_ge(s[("x1_done", "x2_done", "y_done")[k]], n - NT)
                pool.tensor_tensor(rstd[:, k, t:t + 1], veps[:, k, t:t + 1], half_power[:, t:t + 1], ALU.pow)\
                    .then_inc(rstd_done[k], 1)

            for step in steps():
                name, b, i = step
                if name == "maxrow":
                    pool.wait_ge(ld["x"], 32)
                    for t in range(NT):
                        last = pool.tensor_tensor(x_bo[:, NT * b + t, :], x_bo[:, NT * b + t, :], bo_all[:, :],
                                                  ALU.add)
                    last.then_inc(s["x_bo_done"], 1)
                elif name == "probs":
                    if i % UNITS != 1:
                        pool.wait_ge(s["exp_done"], UNITS * G * b + i + 1)
                        block_p = probs[:, i, :].rearrange("p (h q) -> p h q", h=R)
                        pool.affine_select(out=block_p, in_=block_p, compare_op=ALU.is_ge, fill=0.0, base=0,
                                           pattern=[[0, R], [1, P]], channel_multiplier=-1)\
                            .then_inc(s["masked_done"], 1)
                elif name == "wo":
                    power(0, b, i)
                elif name == "expert":
                    n = E * b + i
                    if n == 0:
                        pool.wait_ge(s["route_ge"], E)
                        pool.wait_ge(s["route_done"], E - 2)
                    wait_shared(pool, step)
                    for k in range(ND):
                        last = pool.tensor_tensor(sq[:, n % 2, k, :], sq[:, n % 2, k, :],
                                                  route[:, i, b * S:(b + 1) * S], ALU.mult)
                    last.then_inc(s["sqr_done"], 1)
                elif name == "down" and i == E - 1:
                    for t in range(NT):
                        power(1, b, t)
                elif name == "mix":
                    n = NT * b + i
                    wait_shared(pool, ("gate", b, i))
                    pool.wait_ge(s["x2_done"], n + 1)
                    if b:
                        wait_shared(pool, ("ffn", b - 1, i))
                    pool.tensor_tensor(moe_x[:, i, :], moe[:, i, :], x2[:, i, :], ALU.add)\
                        .then_inc(s["moe_x_done"], 1)
                elif name == "ffn":
                    power(2, b, i)


def rope_tables():
    inv = (1.0 / np.float32(1000000.0) ** (np.arange(0, HD, 2, dtype=np.float32) / np.float32(HD))).astype(np.float32)
    ang = np.arange(S, dtype=np.float32)[None, :] * inv[:, None]
    cos = np.concatenate([np.cos(ang), np.cos(ang)]).astype(np.float32)
    sin = np.concatenate([-np.sin(ang), np.sin(ang)]).astype(np.float32)
    k = np.concatenate([np.repeat(cos, G, 0), np.repeat(sin, G, 0)])
    return np.repeat(cos, HB, 0), np.repeat(sin, HB, 0), k


def by_dim(w, heads):
    w = w.reshape(w.shape[0], heads, HD)
    both = w, np.concatenate([w[:, :, HD // 2:], w[:, :, :HD // 2]], -1)
    return [v.transpose(0, 2, 1).reshape(w.shape[0], -1) for v in both]


def qk_columns(wq, wk):
    blocks = by_dim(wk, G)
    for i in range(NQB):
        blocks += by_dim(wq[:, i * P:(i + 1) * P], HB)
    return np.concatenate(blocks, 1)


def kernel(x, itok_BxS_13_99985, ctx_2048, L0_attn_Wq, L0_attn_bq, L0_attn_Wk, L0_attn_bk, L0_attn_Wv,
           L0_attn_bv, L0_attn_Wo, L0_attn_bo, L0_ffn_W_up, L0_ffn_W_down, L0_ffn_W_gate, L0_ffn_W_expert):
    import ml_dtypes
    import concourse.bacc as bacc
    from concourse.bass_utils import run_bass_kernel_spmd as run

    x, tok, ctx = (np.asarray(v) for v in (x, itok_BxS_13_99985, ctx_2048))
    wq, bq, wk, bk, wv, bv, wo, bo = (np.asarray(v) for v in (
        L0_attn_Wq, L0_attn_bq, L0_attn_Wk, L0_attn_bk, L0_attn_Wv, L0_attn_bv, L0_attn_Wo, L0_attn_bo))
    w_up, w_dn, w_gate, w_exp = (np.asarray(v) for v in (
        L0_ffn_W_up, L0_ffn_W_down, L0_ffn_W_gate, L0_ffn_W_expert))
    cos, sin, rope_k = rope_tables()
    mask = np.where(np.arange(P)[None, :] > np.arange(P)[:, None], MASK, 0.0)
    arrays = {
        "x": x.reshape(B * S, D),
        "x_t": x.reshape(B * S, D).T,
        "tok": tok,
        "w_qk": qk_columns(wq, wk),
        "b_qk": qk_columns(bq[None], bk[None]).reshape(5, P).T,
        "w_v": wv, "b_v": bv, "w_o": wo, "b_o": bo,
        "w_ex": ctx.transpose(2, 0, 1).reshape(D, E * D),
        "w_up": w_up.T,
        "w_gx": np.concatenate([w_exp, w_gate.T], 1),
        "w_dn": w_dn.T,
        "cos": cos, "sin": sin, "rope_k": rope_k,
        "ident": np.eye(P, dtype=np.float32),
        "ident_bf": np.eye(P, dtype=np.float32).astype(ml_dtypes.bfloat16),
        "causal": np.tile(mask, (1, R)).astype(ml_dtypes.bfloat16),
    }
    arrays = {"in_" + k: np.ascontiguousarray(v) for k, v in arrays.items()}
    nc = bacc.Bacc("TRN2", target_bir_lowering=False, num_devices=1)
    a = {k[3:]: nc.dram_tensor(k, v.shape, mybir.dt.from_np(v.dtype), kind="ExternalInput").ap()
         for k, v in arrays.items()}
    a["out"] = nc.dram_tensor("out", (B * S, D), F32, kind="ExternalOutput").ap()
    decoder_layer(nc, a)
    r = run(nc, [arrays], core_ids=[0])
    return r.results[0]["out"].reshape(B, S, D)
```

```python
from contextlib import ExitStack

import numpy as np

import concourse.bass as bass
from concourse import mybir

F32 = mybir.dt.float32
F32R = mybir.dt.float32r
BF16 = mybir.dt.bfloat16
I32 = mybir.dt.int32
ALU = mybir.AluOpType
ACT = mybir.ActivationFunctionType
AX = mybir.AxisListType

P = 128
B, S, D = 4, 256, 256
NT = S // P
ND = D // P
H, G = 16, 4
R = H // G
HD = D // H
KVW = G * HD
E = 4
VOCAB = 12500
TPE = VOCAB // E
NG = 8
EPS = 1e-5
MASK = -4.0e9
SCALE = float(HD) ** -0.5
WARMUPS = 2
QPARTS = (0, 0, 0, 1, 1, 2)
KPARTS = (0, 1, 2, 0, 1, 0)
NPART = len(QPARTS)
KQ = NPART * HD
HB = P // HD
NQB = H // HB
UNITS = 3
VW = 2 * HD


ORDER = {
    "sync": ((
        ("load_late", 0, 0), ("move_high", 0, 0), ("move_high", 0, 1), ("move_mid", 0, 0), ("move_mid", 0, 1),
        ("move", 0, 0), ("move", 0, 1), ("move", 0, 2), ("move_mid", 0, 2), ("move_high", 0, 2),
        ("fetch", 2, 0), ("move_mid", 1, 0), ("move_high", 1, 0), ("move_high", 1, 1), ("move_mid", 1, 1),
        ("move", 1, 0), ("move_max", 0, 0), ("move", 1, 1), ("fetch", 3, 0), ("move_mid", 1, 2),
        ("move", 1, 2), ("move_high", 1, 2), ("load_late", 0, 1),
    ), (
        ("move", 2, 0), ("move", 2, 1), ("move_max", 1, 0), ("move", 2, 2), ("store", -2, 0),
        ("store", -2, 1),
    )),
    "tensor": ((
        ("project", 0, 0), ("project", 0, 1), ("project", 0, 2), ("fill", 0, 0), ("fill", 0, 1),
        ("project", 0, 3), ("project", 1, 0), ("project", 1, 1), ("project", 1, 2), ("fill", 0, 2),
        ("fill", 0, 3), ("fill", 0, 4), ("fill", 0, 5), ("max", 0, 0), ("max", 0, 1), ("fill", 0, 6),
        ("max", 0, 2), ("max", 0, 3), ("max", 0, 4), ("max", 0, 5), ("max", 0, 6), ("max", 0, 7),
        ("max", 0, 8), ("max", 0, 9), ("max", 0, 10), ("project", 1, 3), ("max", 0, 11), ("fill", 0, 7),
        ("maxrow", 0, 0),
    ), (
        ("warm", -2, 0), ("warm", -2, 1), ("heads", -1, 0), ("heads", -1, 1), ("project", 2, 0),
        ("project", 2, 1), ("x2t", -2, 0), ("probs", 0, 0), ("probs", 0, 1), ("attnt", -1, 0), ("max", 1, 0),
        ("attnt", -1, 1), ("x2t", -2, 1), ("wo", -1, 0), ("wo", -1, 1), ("gate", -2, 0), ("probs", 0, 2),
        ("max", 1, 1), ("probs", 0, 3), ("max", 1, 2), ("up", -2, 0), ("x1t", -1, 0), ("probs", 0, 4),
        ("probs", 0, 5), ("x1t", -1, 1), ("max", 1, 3), ("max", 1, 4), ("gate", -2, 1), ("ffn", -2, 0),
        ("probs", 0, 6), ("expert", -1, 0), ("expert", -1, 1), ("project", 2, 2), ("max", 1, 5),
        ("probs", 0, 7), ("ffn", -2, 1), ("max", 1, 6), ("probs", 0, 8), ("expert", -1, 2), ("expert", -1, 3),
        ("max", 1, 7), ("max", 1, 8), ("probs", 0, 9), ("down", -1, 0), ("max", 1, 9), ("probs", 0, 10),
        ("down", -1, 1), ("max", 1, 10), ("probs", 0, 11), ("max", 1, 11), ("down", -1, 2), ("down", -1, 3),
        ("maxrow", 1, 0), ("pv", 0, 0), ("pv", 0, 1), ("project", 2, 3),
    )),
    "scalar": ((
        ("whigh", 0, 0), ("xt_high", 0, 0), ("whigh", 0, 1), ("whigh", 0, 2), ("xt_high", 1, 0),
        ("high", 0, 0), ("high", 0, 1), ("high", 0, 2), ("mid", 0, 0), ("mid", 0, 1), ("high", 1, 0),
        ("mid", 0, 2), ("high", 1, 1), ("high", 1, 2), ("mid", 1, 0), ("xt_high", 2, 0), ("mid", 1, 1),
        ("mid", 1, 2), ("negate", 0, 0),
    ), (
        ("x2t_high", -2, 0), ("w_high", -1, 4), ("attn_t", -1, 0), ("high", 2, 0), ("attn_t", -1, 1),
        ("x2t_high", -2, 1), ("exp", 0, 0), ("exp", 0, 1), ("exp", 0, 2), ("exp", 0, 3), ("gate_exp", -2, 0),
        ("relu", -2, 0), ("x1t_high", -1, 0), ("w_high", -1, 5), ("x1t_high", -1, 1), ("exp", 0, 4),
        ("gate_exp", -2, 1), ("xt_high", 3, 0), ("exp", 0, 5), ("high", 2, 1), ("mid", 2, 0), ("exp", 0, 6),
        ("silu", -1, 0), ("silu", -1, 1), ("exp", 0, 7), ("silu", -1, 2), ("mid", 2, 1), ("exp", 0, 8),
        ("exp", 0, 9), ("silu", -1, 3), ("exp", 0, 10), ("exp", 0, 11), ("w_high", 0, 0), ("negate", 1, 0),
        ("w_high", 0, 1), ("w_high", 0, 2), ("heads_t", 0, 0), ("high", 2, 2), ("heads_t", 0, 1),
        ("mid", 2, 2), ("w_high", 0, 3),
    )),
    "vector": ((
        ("wlow", 0, 0), ("xt_low", 0, 0), ("wlow", 0, 1), ("wlow", 0, 2), ("rope", 0, 0), ("rope", 0, 1),
        ("rope", 0, 2), ("rest", 0, 0), ("rest", 0, 1), ("value", 0, 0), ("rope", 1, 0), ("rest", 0, 2),
        ("rope", 1, 1), ("rope", 1, 2), ("rest", 1, 0), ("reduce", 0, 0), ("reduce", 0, 1), ("reduce", 0, 2),
        ("reduce", 0, 3), ("reduce", 0, 4), ("reduce", 0, 5), ("reduce", 0, 6), ("reduce", 0, 7),
        ("reduce", 0, 8), ("rest", 1, 1), ("reduce", 0, 9), ("rest", 1, 2), ("reduce", 0, 10),
        ("reduce", 0, 11), ("value", 1, 0),
    ), (
        ("attn", -1, 0), ("attn", -1, 1), ("x2t_low", -2, 0), ("x2t_low", -2, 1), ("rope", 2, 0),
        ("rope", 2, 1), ("reduce", 1, 0), ("stats1", -1, 0), ("stats1", -1, 1), ("norm1", -1, 0),
        ("gate_top", -2, 0), ("reduce", 1, 1), ("norm1", -1, 1), ("reduce", 1, 2), ("x1t_low", -1, 0),
        ("x1t_low", -1, 1), ("mix", -2, 0), ("rest", 2, 0), ("gate_top", -2, 1), ("mix", -2, 1),
        ("routing", -1, 0), ("routing", -1, 1), ("reduce", 1, 3), ("reduce", 1, 4), ("rest", 2, 1),
        ("routing", -1, 2), ("stats3", -2, 0), ("routing", -1, 3), ("routing", -1, 4), ("routing", -1, 5),
        ("reduce", 1, 5), ("reduce", 1, 6), ("hid", -1, 0), ("reduce", 1, 7), ("hid", -1, 1),
        ("reduce", 1, 8), ("stats3", -2, 1), ("reduce", 1, 9), ("hid", -1, 2), ("norm3", -2, 0),
        ("reduce", 1, 10), ("reduce", 1, 11), ("hid", -1, 3), ("rope", 2, 2), ("norm3", -2, 1),
        ("stats2", -1, 0), ("rest", 2, 2), ("norm2", -1, 0), ("norm2", -1, 1), ("value", 2, 0),
    )),
    "gpsimd": ((
        ("xt_low", 1, 0), ("low", 0, 0), ("low", 0, 1), ("low", 0, 2), ("xt_low", 2, 0), ("low", 1, 0),
        ("low", 1, 1), ("low", 1, 2),
    ), (
        ("x_bo", -1, 0), ("power1", -1, 0), ("power1", -1, 1), ("causal", 0, 0), ("causal", 0, 2),
        ("causal", 0, 3), ("causal", 0, 5), ("causal", 0, 6), ("low", 2, 0), ("route", -1, 0),
        ("power3", -2, 0), ("route", -1, 1), ("causal", 0, 8), ("route", -1, 2), ("causal", 0, 9),
        ("route", -1, 3), ("w_low", -1, 4), ("low", 2, 1), ("causal", 0, 11), ("w_low", -1, 5),
        ("xt_low", 3, 0), ("w_low", 0, 0), ("w_low", 0, 1), ("w_low", 0, 2), ("power3", -2, 1),
        ("w_low", 0, 3), ("power2", -1, 0), ("power2", -1, 1), ("low", 2, 2),
    )),
}
ONCE = ("w_high", "w_low", "routing")


def steps(engine):
    front, per_round = ORDER[engine]
    yield from front
    for b in range(B + 2):
        for name, distance, part in per_round:
            if 0 <= b + distance < (1 if name in ONCE else B):
                yield name, b + distance, part


SHARED = 3
SHARED_USES = {"project": 1, "maxrow": 1, "pv": 1, "heads": 1, "attnt": 1, "wo": 1, "x1t": 1, "expert": 1, "x2t": 1,
               "up": 1, "gate": 1, "ffn": 1}


def shared_use():
    n, first = 0, {}
    for s in steps("tensor"):
        first[s] = n
        n += SHARED_USES.get(s[0], 0)
    return first


def decoder_layer(nc, a):
    first_use = shared_use()
    with ExitStack() as ctx:
        def sb(name, shape, dt=F32):
            return ctx.enter_context(nc.sbuf_tensor(name, shape, dt))

        def bank(name, shape):
            return ctx.enter_context(nc.psum_tensor(name, shape, F32))

        def sem(name):
            return ctx.enter_context(nc.semaphore(name))

        ident = sb("ident", [P, P])
        masks = sb("masks", [P, (R + 1) * P], BF16)
        ident_bf = masks[:, 0:P]
        causal = masks[:, P:].rearrange("p (r k) -> p r k", r=R)
        tabs = sb("tabs", [P, 3 * S + 1 + NQB])
        rope_k = tabs[:, 0:S]
        cos, sin = tabs[:, S:2 * S], tabs[:, 2 * S:3 * S]
        b_qk = tabs[:, 3 * S:]
        w_qk = sb("w_qk", [P, ND, (1 + NQB) * P])
        w_qk_hi = sb("w_qk_hi", [P, ND, (1 + NQB) * P], F32R)
        w_qk_lo = sb("w_qk_lo", [P, ND, (1 + NQB) * P], F32R)
        w_v = sb("w_v", [P, ND, KVW])
        bv_all = sb("bv_all", [P, NT, KVW])
        w_o = sb("w_o", [P, ND, D])
        bo_all = sb("bo_all", [P, D])
        w_ex = sb("w_ex", [P, ND, E, D])
        w_ex_hi, w_ex_lo = sb("w_ex_hi", [P, ND, E, D], F32R), sb("w_ex_lo", [P, ND, E, D], F32R)
        w_up = sb("w_up", [P, ND, D])
        w_up_hi, w_up_lo = sb("w_up_hi", [P, ND, D], F32R), sb("w_up_lo", [P, ND, D], F32R)
        w_gx = sb("w_gx", [P, ND, D + NG])
        w_gx_hi, w_gx_lo = sb("w_gx_hi", [P, ND, D + NG], F32R), sb("w_gx_lo", [P, ND, D + NG], F32R)
        w_dn = sb("w_dn", [P, ND, D])
        half_power = sb("half_power", [P, NT])
        route = sb("route", [P, E, B * S], BF16)
        x_bo = sb("x_bo", [P, B * NT, D])
        xt = sb("xt", [P, ND, 2, S])
        xt_hi, xt_lo = sb("xt_hi", [P, ND, 2, S], F32R), sb("xt_lo", [P, ND, 2, S], F32R)
        rc, rs = sb("rc", [P, 2, S]), sb("rs", [P, 2, S])
        qk_rot, qk_rest = sb("qk_rot", [P, 3, S]), sb("qk_rest", [P, 3, S])
        qk_parts = sb("qk_parts", [P, 2, 3, 3, S], BF16)
        q_st = sb("q_st", [KQ + 1, 2, H, S], BF16)
        k_st = sb("k_st", [KQ + 1, 3, G, S], BF16)
        v_st = sb("v_st", [P, 2, NT, G, VW])
        mx = sb("mx", [P, 2, NT, H])
        neg_mx = sb("neg_mx", [H, 2, S], BF16)
        probs = sb("probs", [P, UNITS * G, R * P])
        heads_t = sb("heads_t", [P, NT, R * P])
        rden = sb("rden", [P, NT, R, G])
        attn = sb("attn", [P, NT, D])
        attn_t = sb("attn_t", [P, NT, ND, P])
        z = sb("z", [P, 3, NT, D])
        stats = sb("stats", [P, 3, NT, 6])
        mv = sb("mv", [P, 3, NT, 2])
        veps, rstd = sb("veps", [P, 3, NT]), sb("rstd", [P, 3, NT])
        x1, x2 = sb("x1", [P, NT, D]), sb("x2", [P, NT, D])
        x1t_hi, x1t_lo = sb("x1t_hi", [P, ND, S], F32R), sb("x1t_lo", [P, ND, S], F32R)
        x2t_hi, x2t_lo = sb("x2t_hi", [P, ND, S], F32R), sb("x2t_lo", [P, ND, S], F32R)
        th, sq = sb("th", [P, 2, ND, S]), sb("sq", [P, 2, ND, S])
        hid = sb("hid", [P, 2, ND, S])
        tok = hid[:, :, :, :].rearrange("p a k q -> p (a k q)").bitcast(I32)
        up_t = sb("up_t", [P, ND, S])
        top = sb("top", [P, NT, 8])
        gd, ge, gs, gr, gw, gt = (sb(n, [P, NT]) for n in ("gd", "ge", "gs", "gr", "gw", "gt"))
        moe, moe_x = sb("moe", [P, NT, D]), sb("moe_x", [P, NT, D])
        y_out = sb("y_out", [P, 2, NT, D])

        max_ps = [bank(f"max_ps{i}", [P, 512]) for i in range(2)]
        sc_ps = [bank(f"sc_ps{i}", [P, 512]) for i in range(2)]
        down_ps = bank("down_ps", [P, NT, D])
        shared = [bank(f"shared{i}", [P, 512]) for i in range(SHARED)]

        ld = {n: sem("ld_" + n) for n in ("w_k", "w_q0", "w_q1", "tabs", "w_v", "mask", "tok", "w_o", "w_ex",
                                          "w_ffn", "x")}
        ld_xt = [sem(f"ld_xt{b}") for b in range(B)]
        names = ("w_qk_hi w_qk_lo xt_hi xt_lo0 xt_lo w_hi w_lo consts pool_consts route_ge "
                 "route_done x_bo_done proj_mm v_mm rope_cos rope_sin rot_done hi_part rest_done mid_part parts_done "
                 "max_mm max_red mxt_mm score_mm exp_done masked_done pv_mm heads_mm "
                 "rden_done attn_mm wo_mm x1_done x1t_mm x1t_hi_done "
                 "gate_mm sq_done sqr_done hid_done down_mm x2_done x2t_mm x2t_hi_done up_mm "
                 "gx_mm top_done gdiff_done gexp_done gsum_done grec_done gw_done moe_x_done ffn_mm "
                 "y_done").split()
        s = {n: sem(n) for n in names}
        z_done, stats_done, mv_done, veps_done, rstd_done = (
            [sem(f"{n}{k}") for k in range(3)] for n in ("z_done", "stats_done", "mv_done", "veps_done", "rstd_done"))
        moved = [[sem(f"moved{i}_{c}") for c in range(2)] for i in range(3)]
        mx_moved = [sem(f"mx_moved{i}") for i in range(2)]
        stored = [sem(f"stored{i}") for i in range(2)]
        shared_read = [sem(f"shared_read{i}") for i in range(SHARED)]

        late_weights = [(w_ex[:, :, e, :], w_ex_hi[:, :, e, :], w_ex_lo[:, :, e, :]) for e in range(E)]
        late_weights += [(w_up[:, :, :], w_up_hi[:, :, :], w_up_lo[:, :, :]),
                         (w_gx[:, :, :], w_gx_hi[:, :, :], w_gx_lo[:, :, :])]
        MOVED = 16 * NPART

        def take_shared(pe, step, k=0):
            n = first_use[step] + k
            if n >= SHARED:
                pe.wait_ge(shared_read[n % SHARED], n // SHARED)
            return shared[n % SHARED]

        def shared_of(step, k=0):
            n = first_use[step] + k
            return shared[n % SHARED], shared_read[n % SHARED], n // SHARED + 1

        def wait_shared(eng, step, k=0):
            _, read, value = shared_of(step, k)
            eng.wait_ge(read, value)

        def three_pass(pe, out, w_hi, w_lo, m_hi, m_lo):
            n = len(w_hi)
            for k in range(n):
                pe.matmul(out, w_hi[k], m_hi[k], start=(k == 0), stop=False)
                pe.matmul(out, w_hi[k], m_lo[k], start=False, stop=False)
                last = pe.matmul(out, w_lo[k], m_hi[k], start=False, stop=(k == n - 1))
            return last

        def xt_low(eng, b, signal, value):
            c = b % 2
            eng.wait_ge(ld_xt[b], 16)
            eng.wait_ge(s["xt_hi"], b + 1)
            eng.tensor_tensor(xt_lo[:, :, c, :], xt[:, :, c, :], xt_hi[:, :, c, :].bitcast(F32),
                              ALU.subtract).then_inc(signal, 1)

        def wait_xt_lo(eng, b):
            eng.wait_ge(s["xt_lo" if b else "xt_lo0"], max(b, 1))

        block = ctx.enter_context(nc.Block())

        @block.sync
        def _(sp):
            def load(dst, src, signal):
                sp.dma_start(dst, src).then_inc(signal, 16)

            def move(b, i, parts):
                for n in range(NPART):
                    part = QPARTS[n] if i else KPARTS[n]
                    if part in parts:
                        rows = slice(n * HD, (n + 1) * HD)
                        if i:
                            dst, src = q_st[rows, b % 2, HB * (i - 1):HB * i, :], qk_parts[:, b % 2, i, part, :]
                        else:
                            dst, src = k_st[rows, b % 3, :, :], qk_parts[0:KVW, b % 2, i, part, :]
                        sp.dma_start(dst, src).then_inc(moved[i][b % 2], 16)

            w_qk_view = a["w_qk"].rearrange("(k p) n -> p k n", p=P)
            load(w_qk[:, :, 0:P], w_qk_view[:, :, 0:P], ld["w_k"])
            xt_view = a["x_t"].rearrange("(k p) (b s) -> p k b s", p=P, b=B)
            load(xt[:, :, 0, :], xt_view[:, :, 0, :], ld_xt[0])
            load(w_qk[:, :, P:2 * P], w_qk_view[:, :, P:2 * P], ld["w_q0"])
            load(tabs[:, :], a["tabs"], ld["tabs"])
            load(w_qk[:, :, 2 * P:3 * P], w_qk_view[:, :, 2 * P:3 * P], ld["w_q1"])
            load(xt[:, :, 1, :], xt_view[:, :, 1, :], ld_xt[1])
            load(w_v[:, :, :], a["w_v"].rearrange("(k p) n -> p k n", p=P), ld["w_v"])
            load(bv_all[:, :, :], a["b_v"].rearrange("(o t n) -> o t n", o=1, t=1).to_broadcast([P, NT, KVW]),
                 ld["w_v"])
            load(masks[:, :], a["masks"], ld["mask"])
            load(ident[:, :], a["ident"], ld["mask"])

            for step in steps("sync"):
                name, b, i = step
                c = b % 2
                if name == "fetch":
                    sp.wait_ge(s["v_mm"], b - 1)
                    wait_xt_lo(sp, b - 2)
                    load(xt[:, :, c, :], xt_view[:, :, b, :], ld_xt[b])
                elif name in ("move_high", "move_mid"):
                    sp.wait_ge(s["hi_part" if name == "move_high" else "mid_part"], 3 * b + i + 1)
                    move(b, i, (0,) if name == "move_high" else (1,))
                elif name == "move":
                    sp.wait_ge(s["parts_done"], 3 * b + i + 1)
                    read = (UNITS * G * (b - 2), UNITS * G * (b - 2) + UNITS * G // 2, UNITS * G * (b - 1))[i]
                    if b >= (3, 2, 2)[i]:
                        sp.wait_ge(s["score_mm"], read)
                    move(b, i, (2,) if b < 2 else (0, 1, 2))
                elif name == "load_late" and i == 0:
                    load(w_ex[:, :, :, :], a["w_ex"].rearrange("(k p) (e f) -> p k e f", p=P, e=E), ld["w_ex"])
                elif name == "load_late":
                    load(x_bo[:, :, :], a["x"].rearrange("(t p) d -> p t d", p=P), ld["x"])
                    load(bo_all[:, :], a["b_o"].rearrange("(o n) -> o n", o=1).to_broadcast([P, D]), ld["x"])
                    load(w_up[:, :, :], a["w_up"].rearrange("(k p) n -> p k n", p=P), ld["w_ffn"])
                    load(w_gx[:, :, :], a["w_gx"].rearrange("(k p) n -> p k n", p=P), ld["w_ffn"])
                    load(w_dn[:, :, :], a["w_dn"].rearrange("(k p) n -> p k n", p=P), ld["w_ffn"])
                    load(w_o[:, :, :], a["w_o"].rearrange("(k p) n -> p k n", p=P), ld["w_o"])
                elif name == "move_max":
                    wait_shared(sp, ("maxrow", b, 0))
                    sp.dma_start(q_st[KQ:KQ + 1, c, :, :], neg_mx[:, c, :]).then_inc(mx_moved[c], 16)
                elif name == "store":
                    sp.wait_ge(s["y_done"], NT * b + i + 1)
                    t = NT * b + i
                    sp.dma_start(a["out"][t * P:(t + 1) * P, :], y_out[:, c, i, :]).then_inc(stored[c], 16)
            sp.wait_ge(stored[0], 16 * NT * 2)
            sp.wait_ge(stored[1], 16 * NT * 2)

        @block.tensor
        def _(pe):
            pe.wait_ge(s["consts"], 1)
            for n in range(WARMUPS):
                pe.matmul(sc_ps[0][:, :], v_st[:, 0, 0, :, :], v_st[:, :, :, :, :], start=True, stop=True)

            for step in steps("tensor"):
                name, b, i = step
                c = b % 2
                if name == "project":
                    ps = take_shared(pe, step)
                    if i < 3:
                        pe.wait_ge(s["w_qk_lo"], i + 1)
                        wait_xt_lo(pe, b)
                        cols = slice(i * P, (i + 1) * P)
                        last = three_pass(pe, ps[:, 0:S],
                                          [w_qk_hi[:, k, cols] for k in range(ND)],
                                          [w_qk_lo[:, k, cols] for k in range(ND)],
                                          [xt_hi[:, k, c, :] for k in range(ND)],
                                          [xt_lo[:, k, c, :] for k in range(ND)])
                        last.then_inc(s["proj_mm"], 1)
                    else:
                        pe.wait_ge(ld["w_v"], 32)
                        pe.wait_ge(ld_xt[b], 16)
                        for t in range(NT):
                            for k in range(ND):
                                last = pe.matmul(ps[:, t * KVW:(t + 1) * KVW],
                                                 xt[:, k, c, t * P:(t + 1) * P], w_v[:, k, :],
                                                 start=(k == 0), stop=(k == ND - 1))
                        last.then_inc(s["v_mm"], 1)
                elif name == "max":
                    g, u = divmod(i, UNITS)
                    if i == 0:
                        pe.wait_ge(moved[0][c], MOVED * (b // 2 + 1))
                        pe.wait_ge(moved[1][c], MOVED * (b // 2 + 1))
                        pe.wait_ge(ld["mask"], 32)
                    if i == UNITS * G // 2:
                        pe.wait_ge(moved[2][c], MOVED * (b // 2 + 1))
                    n = UNITS * G * b + i
                    if n >= 2:
                        pe.wait_ge(s["max_red"], n - 1)
                    ps = max_ps[n % 2]
                    if u == 0:
                        out = ps[:, :].rearrange("p (h k) -> p h k", h=R)
                        pe.matmul(out, ident_bf[:, :], causal[:, :, :], start=True, stop=False,
                                  skip_group_check=True)
                        hs, q0, nk = range(R), 0, P
                    else:
                        out = ps[:, :].rearrange("p (h k) -> p h k", h=2)
                        pe.matmul(out[:, :, P:S], ident_bf[:, :], causal[:, 0:2, :],
                                  start=True, stop=False, skip_group_check=True)
                        hs, q0, nk = range(2 * (u - 1), 2 * u), P, S
                    for m, h in enumerate(hs):
                        last = pe.matmul(out[:, m, :], q_st[0:KQ, c, R * g + h, q0:q0 + P],
                                         k_st[0:KQ, b % 3, g, 0:nk], start=False, stop=(h == hs[-1]),
                                         skip_group_check=True)
                    last.then_inc(s["max_mm"], 1)
                elif name == "fill":
                    pe.wait_ge(ld["w_q1"], 16)
                    pe.matmul(sc_ps[0][:, 0:3 * P], w_qk[:, 0, 0:P], w_qk[:, 0, 0:3 * P], start=True, stop=True)
                elif name == "warm":
                    if b == B - 1:
                        for _ in range(WARMUPS):
                            pe.matmul(max_ps[0][:, 0:D], ident[:, :], w_dn[:, 0, :], start=True, stop=True)
                elif name == "maxrow":
                    ps = take_shared(pe, step)
                    pe.wait_ge(s["max_red"], UNITS * G * (b + 1))
                    for t in range(NT):
                        last = pe.transpose(ps[0:H, t * P:(t + 1) * P], mx[:, c, t, :], ident[:, :])
                    last.then_inc(s["mxt_mm"], 1)
                elif name == "probs":
                    if i == 0:
                        pe.wait_ge(mx_moved[c], 16 * (b // 2 + 1))
                        pe.wait_ge(s["pool_consts"], 1)
                    g, u = divmod(i, UNITS)
                    t, k = ((0, 0), (1, 0), (1, 1))[u]
                    n = UNITS * G * b + i
                    if n >= 2:
                        pe.wait_ge(s["exp_done"], n - 1)
                    pe.matmul(sc_ps[n % 2][:, :], k_st[:, b % 3, g, k * P:(k + 1) * P],
                              q_st[:, c, R * g:R * (g + 1), t * P:(t + 1) * P],
                              start=True, stop=True).then_inc(s["score_mm"], 1)
                elif name == "pv":
                    ps = take_shared(pe, step)
                    wait_shared(pe, ("project", b, 3))
                    pe.wait_ge(s["exp_done"], UNITS * G * (b + 1))
                    pe.wait_ge(s["masked_done"], 2 * G * (b + 1))
                    for k in range(i + 1):
                        for g in range(G):
                            last = pe.matmul(ps[32 * g:32 * g + VW, :], v_st[:, c, k, g, :],
                                             probs[:, UNITS * g + i + k, :], start=(k == 0), stop=(k == i),
                                             tile_position=(0, 32 * g))
                    last.then_inc(s["pv_mm"], 1)
                elif name == "heads":
                    ps = take_shared(pe, step)
                    wait_shared(pe, ("pv", b, i))
                    for r in range(R):
                        last = pe.transpose(ps[:, r * P:(r + 1) * P], heads_t[:, i, r * P:(r + 1) * P],
                                            ident[:, :])
                    last.then_inc(s["heads_mm"], 1)
                elif name == "attnt":
                    ps = take_shared(pe, step)
                    wait_shared(pe, ("heads", b, i))
                    for k in range(ND):
                        last = pe.transpose(ps[:, k * P:(k + 1) * P], attn[:, i, k * P:(k + 1) * P],
                                            ident[:, :])
                    last.then_inc(s["attn_mm"], 1)
                elif name == "wo":
                    ps = take_shared(pe, step)
                    wait_shared(pe, ("attnt", b, i))
                    pe.wait_ge(ld["w_o"], 16)
                    for k in range(ND):
                        last = pe.matmul(ps[:, 0:D], attn_t[:, i, k, :], w_o[:, k, :],
                                         start=(k == 0), stop=(k == ND - 1))
                    last.then_inc(s["wo_mm"], 1)
                elif name in ("x1t", "x2t"):
                    src = x1 if name == "x1t" else x2
                    ps = take_shared(pe, step)
                    pe.wait_ge(s[name[:2] + "_done"], NT * b + i + 1)
                    for k in range(ND):
                        last = pe.transpose(ps[:, k * P:(k + 1) * P], src[:, i, k * P:(k + 1) * P],
                                            ident[:, :])
                    last.then_inc(s[name + "_mm"], 1)
                elif name == "expert":
                    ps = take_shared(pe, step)
                    pe.wait_ge(s["w_lo"], i + 1)
                    for t in range(NT):
                        wait_shared(pe, ("x1t", b, t))
                    for m in range(ND):
                        cols = slice(m * P, (m + 1) * P)
                        last = three_pass(pe, ps[:, m * S:(m + 1) * S],
                                          [w_ex_hi[:, k, i, cols] for k in range(ND)],
                                          [w_ex_lo[:, k, i, cols] for k in range(ND)],
                                          [x1t_hi[:, k, :] for k in range(ND)],
                                          [x1t_lo[:, k, :] for k in range(ND)])
                    last.then_inc(s["gate_mm"], 1)
                elif name == "down":
                    n = E * b + i
                    pe.wait_ge(s["hid_done"], n + 1)
                    if i == 0 and b:
                        pe.wait_ge(z_done[1], NT * b)
                    for t in range(NT):
                        for k in range(ND):
                            last = pe.matmul(down_ps[:, t, :], hid[:, n % 2, k, t * P:(t + 1) * P],
                                             w_ex[:, k, i, :], start=(i == 0 and k == 0 and t == 0),
                                             stop=(i == E - 1 and k == ND - 1), skip_group_check=True)
                    last.then_inc(s["down_mm"], 1)
                elif name == "up":
                    ps = take_shared(pe, step)
                    pe.wait_ge(s["w_lo"], E + 2)
                    for t in range(NT):
                        wait_shared(pe, ("x2t", b, t))
                    for m in range(ND):
                        cols = slice(m * P, (m + 1) * P)
                        last = three_pass(pe, ps[:, m * S:(m + 1) * S],
                                          [w_up_hi[:, k, cols] for k in range(ND)],
                                          [w_up_lo[:, k, cols] for k in range(ND)],
                                          [x2t_hi[:, k, :] for k in range(ND)],
                                          [x2t_lo[:, k, :] for k in range(ND)])
                    last.then_inc(s["up_mm"], 1)
                elif name == "gate":
                    ps = take_shared(pe, step)
                    pe.wait_ge(s["w_lo"], E + 2)
                    wait_shared(pe, ("x2t", b, i))
                    tt = slice(i * P, (i + 1) * P)
                    three_pass(pe, ps[:, 0:D + NG],
                               [x2t_hi[:, k, tt] for k in range(ND)], [x2t_lo[:, k, tt] for k in range(ND)],
                               [w_gx_hi[:, k, :] for k in range(ND)], [w_gx_lo[:, k, :] for k in range(ND)],
                               ).then_inc(s["gx_mm"], 1)
                elif name == "ffn":
                    ps = take_shared(pe, step)
                    wait_shared(pe, ("up", b, 0))
                    for k in range(ND):
                        last = pe.matmul(ps[:, 0:D], up_t[:, k, i * P:(i + 1) * P], w_dn[:, k, :],
                                         start=(k == 0), stop=(k == ND - 1))
                    last.then_inc(s["ffn_mm"], 1)

        @block.scalar
        def _(act):
            for step in steps("scalar"):
                name, b, i = step
                c = b % 2
                if name == "exp":
                    n = UNITS * G * b + i
                    act.wait_ge(s["score_mm"], n + 1)
                    if b and i == 0:
                        act.wait_ge(s["pv_mm"], NT * b)
                    act.activation(probs[:, i, :], sc_ps[n % 2][:, :], ACT.Exp, scale=SCALE)\
                       .then_inc(s["exp_done"], 1)
                elif name == "whigh":
                    act.wait_ge(ld[("w_k", "w_q0", "w_q1")[i]], 16)
                    act.activation(w_qk_hi[:, :, i * P:(i + 1) * P], w_qk[:, :, i * P:(i + 1) * P], ACT.Copy)\
                       .then_inc(s["w_qk_hi"], 1)
                elif name == "xt_high":
                    act.wait_ge(ld_xt[b], 16)
                    if b >= 2:
                        act.wait_ge(s["proj_mm"], 3 * (b - 1))
                    act.activation(xt_hi[:, :, c, :], xt[:, :, c, :], ACT.Copy).then_inc(s["xt_hi"], 1)
                elif name == "high":
                    act.wait_ge(s["rot_done"], 3 * b + i + 1)
                    if b >= 2:
                        act.wait_ge(moved[i][c], MOVED * (b // 2))
                    rows = slice(0, P if i else KVW)
                    act.activation(qk_parts[rows, c, i, 0, :], qk_rot[rows, i, :], ACT.Copy)\
                       .then_inc(s["hi_part"], 1)
                elif name == "mid":
                    rows = slice(0, P if i else KVW)
                    act.wait_ge(s["rest_done"], 3 * b + i + 1)
                    act.activation(qk_parts[rows, c, i, 1, :], qk_rest[rows, i, :], ACT.Copy)\
                       .then_inc(s["mid_part"], 1)
                elif name == "negate":
                    ps, read, _ = shared_of(("maxrow", b, 0))
                    act.wait_ge(s["mxt_mm"], b + 1)
                    if b >= 2:
                        act.wait_ge(mx_moved[c], 16 * (b // 2))
                    act.activation(neg_mx[:, c, :], ps[0:H, 0:S], ACT.Copy, scale=-1.0).then_inc(read, 1)
                elif name == "w_high":
                    if i == 0:
                        act.wait_ge(ld["w_ex"], 16)
                    if i == E:
                        act.wait_ge(ld["w_ffn"], 48)
                    w, hi, _ = late_weights[i]
                    act.activation(hi, w, ACT.Copy).then_inc(s["w_hi"], 1)
                elif name == "heads_t":
                    n = NT * b + i
                    ps, read, _ = shared_of(("pv", b, i))
                    act.wait_ge(s["pv_mm"], n + 1)
                    if b:
                        act.wait_ge(s["heads_mm"], n - NT + 1)
                    act.activation(heads_t[:, i, :], ps[:, :], ACT.Copy).then_inc(read, 1)
                elif name == "attn_t":
                    n = NT * b + i
                    ps, read, _ = shared_of(("attnt", b, i))
                    act.wait_ge(s["attn_mm"], n + 1)
                    if b:
                        act.wait_ge(s["wo_mm"], n - NT + 1)
                    act.activation(attn_t[:, i, :, :], ps[:, 0:D].rearrange("p (k q) -> p k q", k=ND),
                                   ACT.Copy).then_inc(read, 1)
                elif name in ("x1t_high", "x2t_high"):
                    ps, _, _ = shared_of((name[:3], b, i))
                    act.wait_ge(s[name[:3] + "_mm"], NT * b + i + 1)
                    if b and name == "x1t_high":
                        act.wait_ge(s["gate_mm"], E * b)
                    if b and name == "x2t_high":
                        act.wait_ge(s["gx_mm"], NT * b)
                    hi = x1t_hi if name == "x1t_high" else x2t_hi
                    act.activation(hi[:, :, i * P:(i + 1) * P], ps[:, 0:D].rearrange("p (k q) -> p k q", k=ND),
                                   ACT.Copy).then_inc(s[name[:3] + "_hi_done"], 1)
                elif name == "silu":
                    n = E * b + i
                    ps, read, _ = shared_of(("expert", b, i))
                    act.wait_ge(s["gate_mm"], n + 1)
                    if n >= 2:
                        act.wait_ge(s["hid_done"], n - 1)
                    g = ps[:, :].rearrange("p (m q) -> p m q", m=ND)
                    act.activation(sq[:, n % 2, :, :], g, ACT.Square).then_inc(s["sq_done"], 1)
                    act.activation(th[:, n % 2, :, :], g, ACT.Tanh, scale=0.5).then_inc(read, 1)
                elif name == "relu":
                    ps, read, _ = shared_of(("up", b, 0))
                    act.wait_ge(s["up_mm"], b + 1)
                    if b:
                        act.wait_ge(s["ffn_mm"], NT * b)
                    act.activation(up_t[:, :, :], ps[:, :].rearrange("p (m q) -> p m q", m=ND),
                                   ACT.Relu).then_inc(read, 1)
                elif name == "gate_exp":
                    n = NT * b + i
                    act.wait_ge(s["gdiff_done"], n + 1)
                    if b:
                        act.wait_ge(s["gw_done"], n - NT + 1)
                        act.wait_ge(s["moe_x_done"], n - NT + 1)
                    act.activation(ge[:, i:i + 1], gd[:, i:i + 1], ACT.Exp).then_inc(s["gexp_done"], 1)
                    ps, read, _ = shared_of(("gate", b, i))
                    act.activation(moe[:, i, :], ps[:, 0:D], ACT.Copy).then_inc(read, 1)

        @block.vector
        def _(dve):
            dve.memset(v_st[:, :, :, :, :], 1.0).then_inc(s["consts"], 1)

            def moments(k, b, t):
                n = NT * b + t + 1
                dve.bn_stats(stats[:, k, t, :], z[:, k, t, :]).then_inc(stats_done[k], 1)
                dve.wait_ge(stats_done[k], n)
                if b:
                    dve.wait_ge(rstd_done[k], n - NT)
                dve.bn_aggr(mv[:, k, t, :], stats[:, k, t, :]).then_inc(mv_done[k], 1)

            def normalise(k, b, t, out, signal):
                dve.wait_ge(rstd_done[k], NT * b + t + 1)
                dve.tensor_scalar(out, z[:, k, t, :], mv[:, k, t, 0:1], rstd[:, k, t:t + 1],
                                  ALU.subtract, ALU.mult).then_inc(signal, 1)

            for step in steps("vector"):
                name, b, i = step
                c = b % 2
                if name == "wlow":
                    dve.wait_ge(s["w_qk_hi"], i + 1)
                    cols = slice(i * P, (i + 1) * P)
                    dve.tensor_tensor(w_qk_lo[:, :, cols], w_qk[:, :, cols], w_qk_hi[:, :, cols].bitcast(F32),
                                      ALU.subtract).then_inc(s["w_qk_lo"], 1)
                elif name == "xt_low" and b == 0:
                    xt_low(dve, b, s["xt_lo0"], 1)
                elif name == "rope":
                    ps, read, value = shared_of(("project", b, i))
                    n = 3 * b + i
                    dve.wait_ge(s["proj_mm"], n + 1)
                    dve.wait_ge(ld["tabs"], 16)
                    if n >= 2:
                        dve.wait_ge(s["rot_done"], n - 1)
                    rows = slice(0, P if i else KVW)
                    if i:
                        dve.scalar_tensor_tensor(out=rc[:, n % 2, :], in0=ps[:, 0:S], scalar=b_qk[:, i:i + 1],
                                                 in1=cos, op0=ALU.add, op1=ALU.mult).then_inc(s["rope_cos"], 1)
                        upper, lower = slice(P // 2, P), slice(0, P // 2)
                        dve.scalar_tensor_tensor(out=rs[lower, n % 2, :], in0=ps[upper, 0:S],
                                                 scalar=b_qk[upper, i:i + 1], in1=sin[upper, :],
                                                 op0=ALU.add, op1=ALU.mult).then_inc(s["rope_sin"], 1)
                        dve.scalar_tensor_tensor(out=rs[upper, n % 2, :], in0=ps[lower, 0:S],
                                                 scalar=b_qk[lower, i:i + 1], in1=sin[lower, :],
                                                 op0=ALU.add, op1=ALU.mult).then_inc(read, 1)
                    else:
                        dve.scalar_tensor_tensor(out=rc[0:KVW, n % 2, :], in0=ps[0:KVW, 0:S],
                                                 scalar=b_qk[0:KVW, 0:1], in1=rope_k[0:KVW, :],
                                                 op0=ALU.add, op1=ALU.mult).then_inc(s["rope_cos"], 1)
                        dve.scalar_tensor_tensor(out=rs[0:KVW, n % 2, :], in0=ps[KVW:P, 0:S],
                                                 scalar=b_qk[KVW:P, 0:1], in1=rope_k[KVW:P, :],
                                                 op0=ALU.add, op1=ALU.mult).then_inc(read, 1)
                    dve.wait_ge(s["rope_cos"], n + 1)
                    if i:
                        dve.wait_ge(s["rope_sin"], NQB * b + i)
                    dve.wait_ge(read, value)
                    if b:
                        dve.wait_ge(s["rest_done"], 3 * b + i - 2)
                        dve.wait_ge(s["hi_part"], 3 * b + i - 2)
                    dve.tensor_tensor(qk_rot[rows, i, :], rc[rows, n % 2, :], rs[rows, n % 2, :],
                                      ALU.add).then_inc(s["rot_done"], 1)
                elif name == "value":
                    ps, read, _ = shared_of(("project", b, 3))
                    dve.wait_ge(s["v_mm"], b + 1)
                    dve.wait_ge(ld["w_v"], 32)
                    if b == 0:
                        dve.wait_ge(s["consts"], 1)
                    if b >= 2:
                        dve.wait_ge(s["pv_mm"], NT * (b - 1))
                    dve.tensor_tensor(v_st[:, c, :, :, 0:HD],
                                      ps[:, 0:NT * KVW].rearrange("p (t g d) -> p t g d", t=NT, g=G),
                                      bv_all[:, :, :].rearrange("p t (g d) -> p t g d", g=G),
                                      ALU.add).then_inc(read, 1)
                elif name == "rest":
                    rows = slice(0, P if i else KVW)
                    dve.wait_ge(s["hi_part"], 3 * b + i + 1)
                    if b:
                        dve.wait_ge(s["parts_done"], 3 * b + i - 2)
                        dve.wait_ge(s["mid_part"], 3 * b + i - 2)
                    dve.tensor_tensor(qk_rest[rows, i, :], qk_rot[rows, i, :], qk_parts[rows, c, i, 0, :],
                                      ALU.subtract).then_inc(s["rest_done"], 1)
                elif name == "routing" and i < E:
                    dve.wait_ge(ld["tok"], 16)
                    dve.tensor_scalar(route[:, i, :], tok, float(i * TPE if i else TPE), 0.5,
                                      ALU.is_ge if i else ALU.is_lt, ALU.mult).then_inc(s["route_ge"], 1)
                elif name == "routing":
                    e = i - E + 1
                    dve.wait_ge(s["route_ge"], e + 2)
                    if e > 1:
                        dve.wait_ge(s["route_done"], e - 1)
                    dve.tensor_tensor(route[:, e, :], route[:, e, :], route[:, e + 1, :], ALU.subtract)\
                       .then_inc(s["route_done"], 1)
                elif name == "reduce":
                    if b >= 2 and i == 0:
                        dve.wait_ge(s["mxt_mm"], b - 1)
                    g, u = divmod(i, UNITS)
                    n = UNITS * G * b + i
                    dve.wait_ge(s["max_mm"], n + 1)
                    h, nh = (R * g, R) if u == 0 else (R * g + 2 * (u - 1), 2)
                    dve.tensor_reduce(mx[:, c, int(u > 0), h:h + nh],
                                      max_ps[n % 2][:, :].rearrange("p (h k) -> p h k", h=nh),
                                      AX.X, ALU.max).then_inc(s["max_red"], 1)
                elif name == "attn":
                    n = NT * b + i
                    ps, read, _ = shared_of(("heads", b, i))
                    view = ps[:, :].rearrange("p (r g v) -> p r g v", r=R, g=G)
                    dve.wait_ge(s["heads_mm"], n + 1)
                    dve.reciprocal(rden[:, i, :, :], view[:, :, :, HD]).then_inc(s["rden_done"], 1)
                    dve.wait_ge(s["rden_done"], n + 1)
                    if b:
                        dve.wait_ge(s["attn_mm"], n - NT + 1)
                    dve.tensor_tensor(attn[:, i, :].rearrange("p (g r d) -> p r g d", r=R, g=G),
                                      view[:, :, :, 0:HD],
                                      rden[:, i, :, :].unsqueeze(3).to_broadcast([P, R, G, HD]),
                                      ALU.mult).then_inc(read, 1)
                elif name == "stats1":
                    n = NT * b + i
                    ps, read, value = shared_of(("wo", b, i))
                    dve.wait_ge(s["wo_mm"], n + 1)
                    dve.wait_ge(s["x_bo_done"], b + 1)
                    if b:
                        dve.wait_ge(s["x1_done"], n - NT + 1)
                    dve.tensor_tensor(z[:, 0, i, :], ps[:, 0:D], x_bo[:, n, :], ALU.add).then_inc(read, 1)
                    dve.wait_ge(read, value)
                    moments(0, b, i)
                elif name == "norm1":
                    n = NT * b + i
                    if b:
                        dve.wait_ge(s["x1t_mm"], n - NT + 1)
                        dve.wait_ge(z_done[1], NT * b)
                    normalise(0, b, i, x1[:, i, :], s["x1_done"])
                elif name in ("x1t_low", "x2t_low"):
                    ps, read, _ = shared_of((name[:3], b, i))
                    hi, lo = (x1t_hi, x1t_lo) if name == "x1t_low" else (x2t_hi, x2t_lo)
                    dve.wait_ge(s[name[:3] + "_hi_done"], NT * b + i + 1)
                    dve.tensor_tensor(lo[:, :, i * P:(i + 1) * P], ps[:, 0:D].rearrange("p (k q) -> p k q", k=ND),
                                      hi[:, :, i * P:(i + 1) * P].bitcast(F32), ALU.subtract).then_inc(read, 1)
                elif name == "hid":
                    n = E * b + i
                    wait_shared(dve, ("expert", b, i))
                    dve.wait_ge(s["sqr_done"], n + 1)
                    if n >= 2:
                        dve.wait_ge(s["down_mm"], n - 1)
                    dve.scalar_tensor_tensor(out=hid[:, n % 2, :, :].rearrange("p k q -> p (k q)"),
                                             in0=th[:, n % 2, :, :].rearrange("p k q -> p (k q)"), scalar=1.0,
                                             in1=sq[:, n % 2, :, :].rearrange("p k q -> p (k q)"),
                                             op0=ALU.add, op1=ALU.mult).then_inc(s["hid_done"], 1)
                elif name == "stats2":
                    dve.wait_ge(s["down_mm"], E * (b + 1))
                    dve.wait_ge(s["x1_done"], NT * (b + 1))
                    if b:
                        dve.wait_ge(s["x2_done"], NT * b)
                    for t in range(NT):
                        dve.tensor_tensor(z[:, 1, t, :], down_ps[:, t, :], x1[:, t, :], ALU.add)\
                           .then_inc(z_done[1], 1)
                        dve.wait_ge(z_done[1], NT * b + t + 1)
                        moments(1, b, t)
                elif name == "norm2":
                    n = NT * b + i
                    if b:
                        dve.wait_ge(s["x2t_mm"], n - NT + 1)
                        dve.wait_ge(s["moe_x_done"], n - NT + 1)
                    normalise(1, b, i, x2[:, i, :], s["x2_done"])
                elif name == "gate_top":
                    n = NT * b + i
                    ps, read, _ = shared_of(("gate", b, i))
                    j = slice(i, i + 1)
                    dve.wait_ge(s["gx_mm"], n + 1)
                    dve.max(top[:, i, :], ps[:, D:D + NG]).then_inc(s["top_done"], 1)
                    dve.wait_ge(s["top_done"], n + 1)
                    dve.tensor_tensor(gd[:, j], top[:, i, 1:2], top[:, i, 0:1], ALU.subtract)\
                       .then_inc(s["gdiff_done"], 1)
                elif name == "mix":
                    n = NT * b + i
                    j = slice(i, i + 1)
                    dve.wait_ge(s["gexp_done"], n + 1)
                    dve.tensor_scalar(gs[:, j], ge[:, j], 1.0, None, ALU.add).then_inc(s["gsum_done"], 1)
                    dve.wait_ge(s["gsum_done"], n + 1)
                    dve.reciprocal(gr[:, j], gs[:, j]).then_inc(s["grec_done"], 1)
                    dve.wait_ge(s["grec_done"], n + 1)
                    dve.scalar_tensor_tensor(out=gw[:, j], in0=ge[:, j], scalar=gr[:, j], in1=gr[:, j],
                                             op0=ALU.mult, op1=ALU.add).then_inc(s["gw_done"], 1)
                    dve.wait_ge(s["gw_done"], n + 1)
                    wait_shared(dve, ("gate", b, i))
                    dve.scalar_tensor_tensor(out=moe_x[:, i, :], in0=moe[:, i, :], scalar=gw[:, j],
                                             in1=x2[:, i, :], op0=ALU.mult, op1=ALU.add)\
                       .then_inc(s["moe_x_done"], 1)
                elif name == "stats3":
                    n = NT * b + i
                    ps, read, value = shared_of(("ffn", b, i))
                    dve.wait_ge(s["ffn_mm"], n + 1)
                    dve.wait_ge(s["moe_x_done"], n + 1)
                    if b:
                        dve.wait_ge(s["y_done"], n - NT + 1)
                    dve.tensor_tensor(z[:, 2, i, :], ps[:, 0:D], moe_x[:, i, :], ALU.add).then_inc(read, 1)
                    dve.wait_ge(read, value)
                    moments(2, b, i)
                elif name == "norm3":
                    if b >= 2:
                        dve.wait_ge(stored[c], 16 * NT * (b // 2))
                    normalise(2, b, i, y_out[:, c, i, :], s["y_done"])

        @block.gpsimd
        def _(pool):
            pool.memset(k_st[KQ:KQ + 1, :, :, :], 1.0).then_inc(s["pool_consts"], 1)
            pool.wait_ge(s["pool_consts"], 1)
            pool.memset(half_power[:, :], -0.5).then_inc(s["pool_consts"], 1)
            pool.wait_ge(s["pool_consts"], 2)

            pool.dma_start(tok, a["tok"].rearrange("b s -> (b s)").rearrange("(o n) -> o n", o=1)
                           .to_broadcast([P, B * S])).then_inc(ld["tok"], 16)

            def power(k, b, t):
                n = NT * b + t + 1
                pool.wait_ge(mv_done[k], n)
                pool.tensor_scalar(veps[:, k, t:t + 1], mv[:, k, t, 1:2], EPS, None, ALU.add)\
                    .then_inc(veps_done[k], 1)
                pool.wait_ge(veps_done[k], n)
                if b:
                    pool.wait_ge(s[("x1_done", "x2_done", "y_done")[k]], n - NT)
                pool.tensor_tensor(rstd[:, k, t:t + 1], veps[:, k, t:t + 1], half_power[:, t:t + 1], ALU.pow)\
                    .then_inc(rstd_done[k], 1)

            for step in steps("gpsimd"):
                name, b, i = step
                c = b % 2
                if name == "x_bo":
                    pool.wait_ge(ld["x"], 32)
                    for t in range(NT):
                        last = pool.tensor_tensor(x_bo[:, NT * b + t, :], x_bo[:, NT * b + t, :], bo_all[:, :],
                                                  ALU.add)
                    last.then_inc(s["x_bo_done"], 1)
                elif name == "xt_low" and b:
                    xt_low(pool, b, s["xt_lo"], b)
                elif name == "low":
                    rows = slice(0, P if i else KVW)
                    pool.wait_ge(s["mid_part"], 3 * b + i + 1)
                    pool.tensor_tensor(qk_parts[rows, c, i, 2, :], qk_rest[rows, i, :], qk_parts[rows, c, i, 1, :],
                                       ALU.subtract).then_inc(s["parts_done"], 1)
                elif name == "w_low":
                    pool.wait_ge(s["w_hi"], i + 1)
                    w, hi, lo = late_weights[i]
                    pool.tensor_tensor(lo, w, hi.bitcast(F32), ALU.subtract).then_inc(s["w_lo"], 1)
                elif name == "causal":
                    n = UNITS * G * b + i
                    pool.wait_ge(s["exp_done"], n + 1)
                    block_p = probs[:, i, :].rearrange("p (h q) -> p h q", h=R)
                    pool.affine_select(out=block_p, in_=block_p, compare_op=ALU.is_ge, fill=0.0, base=0,
                                       pattern=[[0, R], [1, P]], channel_multiplier=-1)\
                        .then_inc(s["masked_done"], 1)
                elif name in ("power1", "power2", "power3"):
                    power(int(name[-1]) - 1, b, i)
                elif name == "route":
                    n = E * b + i
                    if b == 0 and i == 0:
                        pool.wait_ge(s["route_ge"], E)
                        pool.wait_ge(s["route_done"], E - 2)
                    pool.wait_ge(s["sq_done"], n + 1)
                    for k in range(ND):
                        last = pool.tensor_tensor(sq[:, n % 2, k, :], sq[:, n % 2, k, :],
                                                  route[:, i, b * S:(b + 1) * S], ALU.mult)
                    last.then_inc(s["sqr_done"], 1)


def rope_tables():
    inv = (1.0 / np.float32(1000000.0) ** (np.arange(0, HD, 2, dtype=np.float32) / np.float32(HD))).astype(np.float32)
    ang = np.arange(S, dtype=np.float32)[None, :] * inv[:, None]
    cos = np.concatenate([np.cos(ang), np.cos(ang)]).astype(np.float32)
    sin = np.concatenate([-np.sin(ang), np.sin(ang)]).astype(np.float32)
    k = np.concatenate([np.repeat(cos, G, 0), np.repeat(sin, G, 0)])
    return np.repeat(cos, HB, 0), np.repeat(np.roll(sin, HD // 2, 0), HB, 0), k


def by_dim(w, heads):
    return w.reshape(w.shape[0], heads, HD).transpose(0, 2, 1).reshape(w.shape[0], -1)


def qk_columns(wq, wk):
    k = by_dim(wk, G)
    blocks = [k, np.roll(k, KVW // 2, 1)] + [by_dim(wq[:, i * P:(i + 1) * P], HB) for i in range(NQB)]
    return np.concatenate(blocks, 1)


def kernel(x, itok_BxS_13_99985, ctx_2048, L0_attn_Wq, L0_attn_bq, L0_attn_Wk, L0_attn_bk, L0_attn_Wv,
           L0_attn_bv, L0_attn_Wo, L0_attn_bo, L0_ffn_W_up, L0_ffn_W_down, L0_ffn_W_gate, L0_ffn_W_expert):
    import ml_dtypes
    import concourse.bacc as bacc
    from concourse.bass_utils import run_bass_kernel_spmd as run

    x, tok, ctx = (np.asarray(v) for v in (x, itok_BxS_13_99985, ctx_2048))
    wq, bq, wk, bk, wv, bv, wo, bo = (np.asarray(v) for v in (
        L0_attn_Wq, L0_attn_bq, L0_attn_Wk, L0_attn_bk, L0_attn_Wv, L0_attn_bv, L0_attn_Wo, L0_attn_bo))
    w_up, w_dn, w_gate, w_exp = (np.asarray(v) for v in (
        L0_ffn_W_up, L0_ffn_W_down, L0_ffn_W_gate, L0_ffn_W_expert))
    cos, sin, rope_k = rope_tables()
    mask = np.where(np.arange(P)[None, :] > np.arange(P)[:, None], MASK, 0.0)
    arrays = {
        "x": x.reshape(B * S, D),
        "x_t": x.reshape(B * S, D).T,
        "tok": tok,
        "w_qk": qk_columns(wq, wk),
        "w_v": wv, "b_v": bv, "w_o": wo, "b_o": bo,
        "w_ex": ctx.transpose(2, 0, 1).reshape(D, E * D),
        "w_up": w_up.T,
        "w_gx": np.concatenate([w_exp, w_gate.T], 1),
        "w_dn": w_dn.T,
        "tabs": np.concatenate([rope_k, cos, sin, qk_columns(bq[None], bk[None]).reshape(1 + NQB, P).T], 1),
        "ident": np.eye(P, dtype=np.float32),
        "masks": np.concatenate([np.eye(P), np.tile(mask, (1, R))], 1).astype(ml_dtypes.bfloat16),
    }
    arrays = {"in_" + k: np.ascontiguousarray(v) for k, v in arrays.items()}
    nc = bacc.Bacc("TRN2", target_bir_lowering=False, num_devices=1)
    a = {k[3:]: nc.dram_tensor(k, v.shape, mybir.dt.from_np(v.dtype), kind="ExternalInput").ap()
         for k, v in arrays.items()}
    a["out"] = nc.dram_tensor("out", (B * S, D), F32, kind="ExternalOutput").ap()
    decoder_layer(nc, a)
    r = run(nc, [arrays], core_ids=[0])
    return r.results[0]["out"].reshape(B, S, D)
```
